# Optimizing a Trainium2 kernel written in Bass

```python
import numpy as np
import jax
import jax.numpy as jnp

def _softmax(x, axis=-1):
    return jax.nn.softmax(x, axis=axis)

def _gelu(x):
    return jax.nn.gelu(x, approximate=True)

def _silu(x):
    return jax.nn.silu(x)

def _sigmoid(x):
    return jax.nn.sigmoid(x)

def _layernorm(x, axis=-1, eps=1e-05):
    m = jnp.mean(x, axis=axis, keepdims=True)
    v = jnp.var(x, axis=axis, keepdims=True)
    return (x - m) / jnp.sqrt(v + eps)

def _scatter_add(tgt, idx, src, axis=0):
    return tgt.at[idx].add(src)

def _segment_sum(src, seg, n):
    return jax.ops.segment_sum(src, seg, n)
kernel_name = 'mk_vit_tower_cls_d2_tok_img1024_r4_a9e36b'

def setup_inputs(seed: int=0):
    np.random.seed(seed)
    _w = jnp.asarray

    def _rec_inputs():
        import jax
        import jax.numpy as jnp
        _rk = jax.random.key(seed)
        x = -0.00150118 + 0.499729 * jax.random.normal(jax.random.fold_in(_rk, 1), (8, 256, 64, 2), jnp.float32)
        cls_tok = 0.02 * jax.random.normal(jax.random.fold_in(_rk, 5), (1, 1, 256), jnp.float32)
        return (x, cls_tok)
    x, cls_tok = _rec_inputs()

    def _L0_tok_setup():
        import jax, jax.numpy as jnp
        import numpy as np
        import math
        H = 256
        N = 64
        CH = 1
        SEQ_L = 256
        key = jax.random.key(seed)
        k1, k2, k3, k4 = jax.random.split(key, 4)
        log_dt = jax.random.uniform(k1, (H,), dtype=jnp.float32, minval=math.log(0.001), maxval=math.log(0.1))
        inv_A_real = jnp.log(0.5 * jnp.ones((H, N), jnp.float32)) + 0.1 * jax.random.normal(k2, (H, N), dtype=jnp.float32)
        A_imag = jnp.broadcast_to(math.pi * jnp.arange(N, dtype=jnp.float32), (H, N)).copy()
        B_ri = jax.random.normal(k3, (H, N, 2), dtype=jnp.float32) * 0.5
        C_ri = jax.random.normal(k4, (CH, H, N, 2), dtype=jnp.float32) * 0.5
        return {'log_dt': log_dt, 'inv_A_real': inv_A_real, 'A_imag': A_imag, 'B_ri': B_ri, 'C_ri': C_ri, 'L': SEQ_L}
    _L0_tok_all = _L0_tok_setup()
    _L0_tok_in = {k: v for k, v in _L0_tok_all.items() if k in ('log_dt', 'inv_A_real', 'A_imag', 'B_ri')}
    del _L0_tok_all

    def _L0_attn_setup():
        import jax, jax.numpy as jnp
        import numpy as np
        D_MODEL = 256
        key = jax.random.key(seed)
        kx, kq, kk, kv = jax.random.split(key, 4)
        B, T, D = (4, 512, D_MODEL)
        bound = np.sqrt(6.0 / D) / np.sqrt(3.0)
        x = jax.random.normal(kx, (B, T, D), dtype=jnp.float32)
        w_q = jax.random.uniform(kq, (D, D), jnp.float32, -bound, bound)
        w_k = jax.random.uniform(kk, (D, D), jnp.float32, -bound, bound)
        w_v = jax.random.uniform(kv, (D, D), jnp.float32, -bound, bound)
        return {'x': x, 'w_q': w_q, 'w_k': w_k, 'w_v': w_v}
    _L0_attn_all = _L0_attn_setup()
    _L0_attn_in = {k: v for k, v in _L0_attn_all.items() if k in ('w_q', 'w_k', 'w_v')}
    del _L0_attn_all

    def _L0_ffn_setup():
        import jax, jax.numpy as jnp
        import numpy as np
        S, B, D = (256, 2, 256)
        E, TOPK = (15, 3)
        F = 256
        FS = 512

        def _uinit(k, shape, out_dim):
            std = out_dim ** (-0.5)
            return jax.random.uniform(k, shape, jnp.float32, -std, std)
        key = jax.random.key(seed)
        ks = jax.random.split(key, 10)
        return {'x': jax.random.normal(ks[0], (S, B, D), jnp.float32), 'gate_w': jax.random.normal(ks[1], (E, D), jnp.float32) * D ** (-0.5), 'fc1_w': _uinit(ks[2], (E, 2 * F, D), 2 * F), 'fc1_b': _uinit(ks[3], (E, 2 * F), 2 * F), 'geglu_mult': jnp.ones((E, F), jnp.float32), 'fc2_w': _uinit(ks[4], (E, D, F), D), 'fc2_b': _uinit(ks[5], (E, D), D), 's_fc1_w': _uinit(ks[6], (2 * FS, D), 2 * FS), 's_fc1_b': _uinit(ks[7], (2 * FS,), 2 * FS), 's_geglu_mult': jnp.ones((FS,), jnp.float32), 's_fc2_w': _uinit(ks[8], (D, FS), D), 's_fc2_b': _uinit(ks[9], (D,), D)}
    _L0_ffn_all = _L0_ffn_setup()
    _L0_ffn_in = {k: v for k, v in _L0_ffn_all.items() if k in ('gate_w', 'fc1_w', 'fc1_b', 'geglu_mult', 'fc2_w', 'fc2_b', 's_fc1_w', 's_fc1_b', 's_geglu_mult', 's_fc2_w', 's_fc2_b')}
    del _L0_ffn_all

    def _L1_attn_setup():
        import jax, jax.numpy as jnp
        import numpy as np
        H = 256
        NH = 16
        HD = H // NH
        BUCKETS = 64
        MAXREL = 128
        SPAN = BUCKETS
        B, S = (2, 512)

        def _log_bucket(rel, bucket_size, max_position):
            sign = jnp.sign(rel).astype(jnp.float32)
            mid = bucket_size // 2
            abs_pos = jnp.where((rel < mid) & (rel > -mid), mid - 1, jnp.abs(rel)).astype(jnp.float32)
            log_pos = jnp.ceil(jnp.log(abs_pos / mid) / np.float32(np.log((max_position - 1) / mid)) * (mid - 1)) + mid
            bucket = jnp.where(abs_pos <= mid, rel.astype(jnp.float32), log_pos * sign)
            return bucket.astype(jnp.int32)

        def _split_heads(x, b, s):
            return x.reshape(b, s, NH, HD).transpose(0, 2, 1, 3)
        key = jax.random.key(seed)
        ks = jax.random.split(key, 10)
        s = 0.02
        return {'hidden_states': jax.random.normal(ks[0], (B, S, H), jnp.float32), 'Wq': jax.random.normal(ks[1], (H, H), jnp.float32) * s, 'bq': jnp.zeros((H,), jnp.float32), 'Wk': jax.random.normal(ks[2], (H, H), jnp.float32) * s, 'bk': jnp.zeros((H,), jnp.float32), 'Wv': jax.random.normal(ks[3], (H, H), jnp.float32) * s, 'bv': jnp.zeros((H,), jnp.float32), 'Wo': jax.random.normal(ks[4], (H, H), jnp.float32) * s, 'bo': jnp.zeros((H,), jnp.float32), 'Wpk': jax.random.normal(ks[5], (H, H), jnp.float32) * s, 'bpk': jnp.zeros((H,), jnp.float32), 'Wpq': jax.random.normal(ks[6], (H, H), jnp.float32) * s, 'bpq': jnp.zeros((H,), jnp.float32), 'rel_emb': jax.random.normal(ks[7], (2 * SPAN, H), jnp.float32) * s, 'ln_g': jnp.ones((H,), jnp.float32), 'ln_b': jnp.zeros((H,), jnp.float32)}
    _L1_attn_all = _L1_attn_setup()
    _L1_attn_in = {k: v for k, v in _L1_attn_all.items() if k in ('Wq', 'bq', 'Wk', 'bk', 'Wv', 'bv', 'Wo', 'bo', 'Wpk', 'bpk', 'Wpq', 'bpq', 'rel_emb', 'ln_g', 'ln_b')}
    del _L1_attn_all

    def _L1_ffn_setup():
        import jax, jax.numpy as jnp
        import numpy as np
        E = 32
        K = 4
        H = 256
        F = 256
        LIMIT = 7.0
        ALPHA = 1.702
        EPS = 1e-05

        def _rmsnorm(x, scale):
            t = x * jax.lax.rsqrt(jnp.mean(x * x, axis=-1, keepdims=True) + EPS)
            return t * scale

        def _swiglu(h):
            glu = jnp.minimum(h[..., ::2], LIMIT)
            lin = jnp.clip(h[..., 1::2], -LIMIT, LIMIT)
            return glu * jax.nn.sigmoid(ALPHA * glu) * (lin + 1.0)
        key = jax.random.key(seed)
        ks = jax.random.split(key, 8)
        B, S = (1, 256)
        x = jax.random.normal(ks[0], (B, S, H), dtype=jnp.float32)
        norm_scale = jnp.ones((H,), dtype=jnp.float32)
        gate_w = jax.random.normal(ks[1], (E, H), dtype=jnp.float32) * 0.02
        gate_b = jnp.zeros((E,), dtype=jnp.float32)
        w1 = jax.random.normal(ks[2], (E, 2 * F, H), dtype=jnp.float32) * 0.02
        b1 = jnp.zeros((E, 2 * F), dtype=jnp.float32)
        w2 = jax.random.normal(ks[3], (E, H, F), dtype=jnp.float32) * 0.02
        b2 = jnp.zeros((E, H), dtype=jnp.float32)
        return {'x': x, 'norm_scale': norm_scale, 'gate_w': gate_w, 'gate_b': gate_b, 'w1': w1, 'b1': b1, 'w2': w2, 'b2': b2}
    _L1_ffn_all = _L1_ffn_setup()
    _L1_ffn_in = {k: v for k, v in _L1_ffn_all.items() if k in ('norm_scale', 'gate_w', 'gate_b', 'w1', 'b1', 'w2', 'b2')}
    del _L1_ffn_all
    return {'x': x, 'cls_tok': cls_tok, 'L0_tok_log_dt': _L0_tok_in['log_dt'], 'L0_tok_inv_A_real': _L0_tok_in['inv_A_real'], 'L0_tok_A_imag': _L0_tok_in['A_imag'], 'L0_tok_B_ri': _L0_tok_in['B_ri'], 'L0_attn_w_q': _L0_attn_in['w_q'], 'L0_attn_w_k': _L0_attn_in['w_k'], 'L0_attn_w_v': _L0_attn_in['w_v'], 'L0_ffn_gate_w': _L0_ffn_in['gate_w'], 'L0_ffn_fc1_w': _L0_ffn_in['fc1_w'], 'L0_ffn_fc1_b': _L0_ffn_in['fc1_b'], 'L0_ffn_geglu_mult': _L0_ffn_in['geglu_mult'], 'L0_ffn_fc2_w': _L0_ffn_in['fc2_w'], 'L0_ffn_fc2_b': _L0_ffn_in['fc2_b'], 'L0_ffn_s_fc1_w': _L0_ffn_in['s_fc1_w'], 'L0_ffn_s_fc1_b': _L0_ffn_in['s_fc1_b'], 'L0_ffn_s_geglu_mult': _L0_ffn_in['s_geglu_mult'], 'L0_ffn_s_fc2_w': _L0_ffn_in['s_fc2_w'], 'L0_ffn_s_fc2_b': _L0_ffn_in['s_fc2_b'], 'L1_attn_Wq': _L1_attn_in['Wq'], 'L1_attn_bq': _L1_attn_in['bq'], 'L1_attn_Wk': _L1_attn_in['Wk'], 'L1_attn_bk': _L1_attn_in['bk'], 'L1_attn_Wv': _L1_attn_in['Wv'], 'L1_attn_bv': _L1_attn_in['bv'], 'L1_attn_Wo': _L1_attn_in['Wo'], 'L1_attn_bo': _L1_attn_in['bo'], 'L1_attn_Wpk': _L1_attn_in['Wpk'], 'L1_attn_bpk': _L1_attn_in['bpk'], 'L1_attn_Wpq': _L1_attn_in['Wpq'], 'L1_attn_bpq': _L1_attn_in['bpq'], 'L1_attn_rel_emb': _L1_attn_in['rel_emb'], 'L1_attn_ln_g': _L1_attn_in['ln_g'], 'L1_attn_ln_b': _L1_attn_in['ln_b'], 'L1_ffn_norm_scale': _L1_ffn_in['norm_scale'], 'L1_ffn_gate_w': _L1_ffn_in['gate_w'], 'L1_ffn_gate_b': _L1_ffn_in['gate_b'], 'L1_ffn_w1': _L1_ffn_in['w1'], 'L1_ffn_b1': _L1_ffn_in['b1'], 'L1_ffn_w2': _L1_ffn_in['w2'], 'L1_ffn_b2': _L1_ffn_in['b2']}

def reference(x, cls_tok, L0_tok_log_dt, L0_tok_inv_A_real, L0_tok_A_imag, L0_tok_B_ri, L0_attn_w_q, L0_attn_w_k, L0_attn_w_v, L0_ffn_gate_w, L0_ffn_fc1_w, L0_ffn_fc1_b, L0_ffn_geglu_mult, L0_ffn_fc2_w, L0_ffn_fc2_b, L0_ffn_s_fc1_w, L0_ffn_s_fc1_b, L0_ffn_s_geglu_mult, L0_ffn_s_fc2_w, L0_ffn_s_fc2_b, L1_attn_Wq, L1_attn_bq, L1_attn_Wk, L1_attn_bk, L1_attn_Wv, L1_attn_bv, L1_attn_Wo, L1_attn_bo, L1_attn_Wpk, L1_attn_bpk, L1_attn_Wpq, L1_attn_bpq, L1_attn_rel_emb, L1_attn_ln_g, L1_attn_ln_b, L1_ffn_norm_scale, L1_ffn_gate_w, L1_ffn_gate_b, L1_ffn_w1, L1_ffn_b1, L1_ffn_w2, L1_ffn_b2):
    import jax
    import jax.numpy as jnp

    def _L0_tok_ref(log_dt, inv_A_real, A_imag, B_ri, C_ri, L):
        import jax, jax.numpy as jnp
        import numpy as np
        import math
        H = 256
        N = 64
        CH = 1
        SEQ_L = 256
        dt = jnp.exp(log_dt)
        A = -jnp.exp(inv_A_real) + 1j * A_imag
        B = B_ri[..., 0] + 1j * B_ri[..., 1]
        C = C_ri[..., 0] + 1j * C_ri[..., 1]
        dtA = A * dt[:, None]
        dA = (1.0 + dtA / 2) / (1.0 - dtA / 2)
        C_term = C * B[None]
        log_dA = jnp.log(dA)
        V = jnp.exp(log_dA[:, :, None] * jnp.arange(L))
        K = 2.0 * jnp.einsum('chn,hnl->chl', C_term, V).real
        return K.astype(jnp.float32)

    def _L0_attn_ref(x, w_q, w_k, w_v):
        import jax, jax.numpy as jnp
        import numpy as np
        D_MODEL = 256
        B, T, D = x.shape
        q = jnp.einsum('btk,kd->btd', x, w_q)
        k = jnp.einsum('btk,kd->btd', x, w_k)
        v = jnp.einsum('btk,kd->btd', x, w_v)
        gamma = 1.0 / jnp.sqrt(jnp.float32(D))
        causal = jnp.tril(jnp.ones((T, T), dtype=bool))
        scores = jnp.einsum('bqd,bkd->bqk', q, k) * gamma
        scores = jnp.where(causal[None, :, :], scores, -jnp.inf)
        a = jax.nn.softmax(scores, axis=-1)
        y = jnp.einsum('bqt,btd->bqd', a, v)
        return y

    def _L0_ffn_ref(x, gate_w, fc1_w, fc1_b, geglu_mult, fc2_w, fc2_b, s_fc1_w, s_fc1_b, s_geglu_mult, s_fc2_w, s_fc2_b):
        import jax, jax.numpy as jnp
        import numpy as np
        S, B, D = (256, 2, 256)
        E, TOPK = (15, 3)
        F = 256
        FS = 512

        def _uinit(k, shape, out_dim):
            std = out_dim ** (-0.5)
            return jax.random.uniform(k, shape, jnp.float32, -std, std)
        s, b, d = x.shape
        xt = x.reshape(-1, d)
        T = xt.shape[0]
        logits = xt @ gate_w.T
        scores = jax.nn.softmax(logits, axis=-1)
        topk_w, topk_idx = jax.lax.top_k(scores, TOPK)
        topk_w = topk_w / (jnp.sum(topk_w, axis=-1, keepdims=True) + 1e-20)
        comb = jnp.zeros((T, E), xt.dtype).at[jnp.arange(T)[:, None], topk_idx].add(topk_w)
        h = jnp.einsum('td,efd->etf', xt, fc1_w) + fc1_b[:, None, :]
        xh, g = (h[..., :F], h[..., F:])
        a = jax.nn.gelu(g, approximate=False) * xh * geglu_mult[:, None, :]
        yexp = jnp.einsum('etf,edf->etd', a, fc2_w) + fc2_b[:, None, :]
        y = jnp.einsum('etd,te->td', yexp, comb)
        hs = xt @ s_fc1_w.T + s_fc1_b
        xs, gs = (hs[..., :FS], hs[..., FS:])
        as_ = jax.nn.gelu(gs, approximate=False) * xs * s_geglu_mult
        ys = as_ @ s_fc2_w.T + s_fc2_b
        return (y + ys).reshape(s, b, d)

    def _L1_attn_ref(hidden_states, Wq, bq, Wk, bk, Wv, bv, Wo, bo, Wpk, bpk, Wpq, bpq, rel_emb, ln_g, ln_b):
        import jax, jax.numpy as jnp
        import numpy as np
        H = 256
        NH = 16
        HD = H // NH
        BUCKETS = 64
        MAXREL = 128
        SPAN = BUCKETS
        B, S = (2, 512)

        def _log_bucket(rel, bucket_size, max_position):
            sign = jnp.sign(rel).astype(jnp.float32)
            mid = bucket_size // 2
            abs_pos = jnp.where((rel < mid) & (rel > -mid), mid - 1, jnp.abs(rel)).astype(jnp.float32)
            log_pos = jnp.ceil(jnp.log(abs_pos / mid) / np.float32(np.log((max_position - 1) / mid)) * (mid - 1)) + mid
            bucket = jnp.where(abs_pos <= mid, rel.astype(jnp.float32), log_pos * sign)
            return bucket.astype(jnp.int32)

        def _split_heads(x, b, s):
            return x.reshape(b, s, NH, HD).transpose(0, 2, 1, 3)
        b, s, _ = hidden_states.shape
        q = _split_heads(hidden_states @ Wq + bq, b, s)
        k = _split_heads(hidden_states @ Wk + bk, b, s)
        v = _split_heads(hidden_states @ Wv + bv, b, s)
        scale = jnp.sqrt(jnp.asarray(HD * 3, jnp.float32))
        scores = jnp.einsum('bhqd,bhkd->bhqk', q, k) / scale
        ids = jnp.arange(s)
        rel = _log_bucket(ids[:, None] - ids[None, :], BUCKETS, MAXREL)
        mu = rel_emb.mean(-1, keepdims=True)
        var = rel_emb.var(-1, keepdims=True)
        re = (rel_emb - mu) / jnp.sqrt(var + 1e-05) * ln_g + ln_b
        pos_k = (re @ Wpk + bpk).reshape(2 * SPAN, NH, HD).transpose(1, 0, 2)
        pos_q = (re @ Wpq + bpq).reshape(2 * SPAN, NH, HD).transpose(1, 0, 2)
        c2p = jnp.einsum('bhqd,hpd->bhqp', q, pos_k)
        c2p_idx = jnp.clip(rel + SPAN, 0, 2 * SPAN - 1)
        c2p = jnp.take_along_axis(c2p, jnp.broadcast_to(c2p_idx[None, None], (b, NH, s, s)), axis=-1) / scale
        p2c = jnp.einsum('bhkd,hpd->bhkp', k, pos_q)
        p2c_idx = jnp.clip(-rel + SPAN, 0, 2 * SPAN - 1)
        p2c = jnp.take_along_axis(p2c, jnp.broadcast_to(p2c_idx[None, None], (b, NH, s, s)), axis=-1)
        p2c = jnp.swapaxes(p2c, -1, -2) / scale
        scores = scores + c2p + p2c
        probs = jax.nn.softmax(scores.astype(jnp.float32), axis=-1).astype(q.dtype)
        ctx = jnp.einsum('bhqk,bhkd->bhqd', probs, v)
        ctx = ctx.transpose(0, 2, 1, 3).reshape(b, s, H)
        return ctx @ Wo + bo

    def _L1_ffn_ref(x, norm_scale, gate_w, gate_b, w1, b1, w2, b2):
        import jax, jax.numpy as jnp
        import numpy as np
        E = 32
        K = 4
        H = 256
        F = 256
        LIMIT = 7.0
        ALPHA = 1.702
        EPS = 1e-05

        def _rmsnorm(x, scale):
            t = x * jax.lax.rsqrt(jnp.mean(x * x, axis=-1, keepdims=True) + EPS)
            return t * scale

        def _swiglu(h):
            glu = jnp.minimum(h[..., ::2], LIMIT)
            lin = jnp.clip(h[..., 1::2], -LIMIT, LIMIT)
            return glu * jax.nn.sigmoid(ALPHA * glu) * (lin + 1.0)
        B, S, _ = x.shape
        t = _rmsnorm(x, norm_scale)
        g = t @ gate_w.T + gate_b
        tf = t.reshape(-1, H)
        gf = g.reshape(-1, E)
        T = tf.shape[0]
        vals, idx = jax.lax.top_k(gf, K)
        w = jax.nn.softmax(vals, axis=-1)
        combine = jnp.zeros((T, E), dtype=tf.dtype).at[jnp.arange(T)[:, None], idx].add(w)
        h1 = jnp.einsum('th,efh->tef', tf, w1) + b1
        h = _swiglu(h1)
        hw = h * combine[:, :, None]
        out = jnp.einsum('tef,ehf->th', hw, w2) + combine @ b2
        return x + out.reshape(B, S, H)
    h = _L0_tok_ref(L0_tok_log_dt, L0_tok_inv_A_real, L0_tok_A_imag, L0_tok_B_ri, x, 256)
    h = jnp.concatenate([jnp.broadcast_to(cls_tok, (h.shape[0], 1, h.shape[2])), h], axis=1)
    h = h + _L0_attn_ref(_layernorm(h, axis=-1), L0_attn_w_q, L0_attn_w_k, L0_attn_w_v)
    h = h + _L0_ffn_ref(_layernorm(h, axis=-1), L0_ffn_gate_w, L0_ffn_fc1_w, L0_ffn_fc1_b, L0_ffn_geglu_mult, L0_ffn_fc2_w, L0_ffn_fc2_b, L0_ffn_s_fc1_w, L0_ffn_s_fc1_b, L0_ffn_s_geglu_mult, L0_ffn_s_fc2_w, L0_ffn_s_fc2_b)
    h = h + _L1_attn_ref(_layernorm(h, axis=-1), L1_attn_Wq, L1_attn_bq, L1_attn_Wk, L1_attn_bk, L1_attn_Wv, L1_attn_bv, L1_attn_Wo, L1_attn_bo, L1_attn_Wpk, L1_attn_bpk, L1_attn_Wpq, L1_attn_bpq, L1_attn_rel_emb, L1_attn_ln_g, L1_attn_ln_b)
    h = h + _L1_ffn_ref(_layernorm(h, axis=-1), L1_ffn_norm_scale, L1_ffn_gate_w, L1_ffn_gate_b, L1_ffn_w1, L1_ffn_b1, L1_ffn_w2, L1_ffn_b2)
    return h

_drawn_inputs = setup_inputs


def setup_inputs(seed=0):
    import zlib

    import numpy as np

    out = dict(_drawn_inputs(seed))
    spreads = {'L0_ffn_geglu_mult': (1.0, 0.6),
     'L0_ffn_s_geglu_mult': (1.0, 0.6),
     'L1_attn_bq': (0.0, 0.8),
     'L1_attn_bk': (0.0, 0.8),
     'L1_attn_bv': (0.0, 0.8),
     'L1_attn_bo': (0.0, 1.235),
     'L1_attn_bpk': (0.0, 2.0),
     'L1_attn_bpq': (0.0, 0.8),
     'L1_attn_ln_g': (1.0, 0.6),
     'L1_attn_ln_b': (0.0, 0.8),
     'L1_ffn_norm_scale': (1.0, 0.6),
     'L1_ffn_gate_b': (0.0, 0.8),
     'L1_ffn_b1': (0.0, 0.8),
     'L1_ffn_b2': (0.0, 2.0)}
    factors = {'L0_attn_w_q': 2.749,
     'L0_attn_w_k': 2.669,
     'L0_ffn_gate_w': 6.136,
     'L0_ffn_fc1_w': 6.676,
     'L0_ffn_fc1_b': 8.0,
     'L0_ffn_fc2_w': 6.679,
     'L0_ffn_fc2_b': 25.496,
     'L0_ffn_s_fc1_w': 6.239,
     'L0_ffn_s_fc1_b': 8.0,
     'L0_ffn_s_fc2_w': 6.225,
     'L0_ffn_s_fc2_b': 20.016,
     'L1_attn_Wq': 8.0,
     'L1_attn_Wk': 8.0,
     'L1_attn_Wv': 8.0,
     'L1_attn_Wo': 6.84,
     'L1_attn_Wpk': 8.0,
     'L1_attn_Wpq': 8.0,
     'L1_attn_rel_emb': 8.0,
     'L1_ffn_gate_w': 5.261,
     'L1_ffn_w1': 8.0,
     'L1_ffn_w2': 8.0}
    for name, (base, spread) in spreads.items():
        noise = np.random.default_rng([zlib.crc32(name.encode()), seed]).standard_normal(out[name].shape)
        drawn = base * np.exp(spread * noise) if base else spread * noise
        out[name] = jnp.asarray(drawn.astype(out[name].dtype))
    for name, factor in factors.items():
        out[name] = (out[name] * factor).astype(out[name].dtype)
    return out
```

```python
from contextlib import ExitStack, contextmanager

import math

import numpy as np

import concourse.bass as bass
from concourse import mybir

B = 8
S = 257
D = 256
P = 128
KC = D // P
TS = 86
IT = 3
SP = IT * TS
NT = B * IT
NTOK = B * SP
STATES = 64
HEADS = 16
HD = D // HEADS
HG = P // HD
SPAN = 64
NBK = 2 * SPAN
BR = 6
CMAX = 3 * BR
CHUNKS = [(n, min(CMAX, SP - n)) for n in range(0, SP, CMAX)]
SLOTS = P // (2 * HD)
BANK = 512
EPS = 1e-5
F = 256
FS = 512
ETILE = 128
E0, K0 = 15, 3
E1, K1 = 32, 4
LIMIT = 7.0
LN2_HIGH = 0.693359375
LN2_LOW = math.log(2.0) - LN2_HIGH


def expert_tiles(experts, picks):
    n = B * S * picks // ETILE + experts
    return -(-n // 4) * 4


F32 = mybir.dt.float32
I32 = mybir.dt.int32
U32 = mybir.dt.uint32
ALU = mybir.AluOpType
ACT = mybir.ActivationFunctionType
AX = mybir.AxisListType


class Own:

    def __init__(self, eng, sem):
        self.eng, self.sem, self.base, self.n = eng, sem, 0, 0

    def __call__(self, ins):
        ins.then_inc(self.sem, 1)
        self.n += 1
        self.eng.wait_ge(self.sem, self.base + self.n)

    @contextmanager
    def loop(self, count, per, first=0):
        start = self.base + self.n
        with self.eng.Fori(first, first + count) as i:
            self.base, self.n = i * per + (start - first * per), 0
            yield i
            assert self.n == per, self.n
        self.base, self.n = start + count * per, 0


def free(eng, sem, n):
    if not isinstance(n, int) or n > 0:
        eng.wait_ge(sem, n)


class Phase:

    def __init__(self, nc, name):
        self.nc, self.name, self.stack, self.sems = nc, name, ExitStack(), []

    def __enter__(self):
        return self

    def __exit__(self, *a):
        self.stack.__exit__(*a)
        self.nc.clear_and_free_semaphores(self.sems)
        self.nc.all_engine_barrier()

    def sb(self, name, shape, dt=F32):
        return self.stack.enter_context(self.nc.sbuf_tensor(f"{self.name}_{name}", shape, dt))

    def ps(self, name, banks=1):
        return self.stack.enter_context(self.nc.psum_tensor(f"{self.name}_{name}", [P, banks, BANK], F32))

    def sem(self, name):
        self.sems.append(self.nc.alloc_semaphore(name=f"{self.name}_{name}"))
        return self.sems[-1]

    def block(self):
        return self.stack.enter_context(self.nc.Block())


def constants_phase(nc, ident):
    with Phase(nc, "const") as ph:
        zeroed, done = ph.sem("zeroed"), ph.sem("done")
        block = ph.block()

        @block.gpsimd
        def _(pool):
            nc.gpsimd.memset(ident[:], 0.0).then_inc(zeroed, 1)
            pool.wait_ge(zeroed, 1)
            nc.gpsimd.affine_select(out=ident[:], in_=ident[:], compare_op=ALU.not_equal, fill=1.0, base=0,
                                    pattern=[[-1, P]], channel_multiplier=1).then_inc(done, 1)
            pool.wait_ge(done, 1)


def s4_phase(nc, h, ident, A):
    NA, NB = D // STATES, STATES
    HH = D // 2
    HZ = HH // 2
    GC = BANK // (NA * B)
    groups = [(z, half, z * HZ + n) for z in range(2) for half in range(2) for n in range(0, HZ, GC)]
    with Phase(nc, "s4") as ph:
        sb, sem = ph.sb, ph.sem
        prm = sb("prm", [P, 5, HH])
        cin = sb("cin", [P, 2, B, HH])
        tmp, n_i = sb("tmp", [P, 10, HH]), sb("n_i", [P, HH], I32)
        pw = sb("pw", [P, 7, 2, HH])
        q = sb("q", [P, 2, NB, HH])
        x = sb("x", [P, 2, NA, B, HH])
        xt = sb("xt", [P, 2, B, HH])
        qt = sb("qt", [P, 2, NB // 2, HZ])
        hT = sb("hT", [NB, NA, NTOK])
        cls = sb("cls", [NB, NA])
        ps = [ph.ps(f"ps{n}") for n in range(4)]
        pt = [ph.ps(f"pt{n}") for n in range(4)]
        ld, c_ld, cl, ex, pwr, own_v, own_p = (sem(n) for n in (
            "params_in", "c_in", "cls_in", "exps", "powers", "own_v", "own_p"))
        qre, qim, xdone, kdone, kcopied_v, kcopied_s, hdone = (sem(n) for n in (
            "qre", "qim", "xdone", "kdone", "kcopied_v", "kcopied_s", "hdone"))
        tdone, tcopied, edge = sem("tdone"), sem("tcopied"), sem("edge")
        levels = 6
        block = ph.block()

        def copy_sums(copy, g):
            _, half, h0 = groups[g]
            c0 = half * HH + h0 + 1
            return copy(hT[:].rearrange("p a (c s) -> p a c s", c=B)[:, :, :, c0:c0 + GC],
                        ps[g % 4][0:NB, 0, :].rearrange("p (h a c) -> p a c h", a=NA, c=B))

        first = len(groups) // 2

        def copied(g):
            if g < first:
                return kcopied_s, g + 1
            return (kcopied_v, (g - first) // 2 + 1) if g % 2 == 0 else (kcopied_s, first + (g - first) // 2 + 1)

        @block.sync
        def _(sp):
            sp.dma_start(prm[:], A["s4_params"]).then_inc(ld, 16)
            sp.dma_start(cin[:], A["s4_c"]).then_inc(c_ld, 16)
            sp.dma_start(cls[:], A["cls"]).then_inc(cl, 16)

        @block.scalar
        def _(act):
            act.wait_ge(ld, 16)
            nc.scalar.activation(tmp[:, 1], prm[:, 1], ACT.Exp).then_inc(ex, 1)
            for g in [*range(first), *range(first + 1, len(groups), 2)]:
                act.wait_ge(kdone, g + 1)
                copy_sums(lambda dst, src: nc.scalar.activation(dst, src, ACT.Copy), g).then_inc(kcopied_s, 1)
            for g in range(12):
                if g % 2:
                    act.wait_ge(tdone, g + 1)
                    nc.scalar.activation(h[:, 2 * g:2 * g + 2, :], pt[g % 4][0:TS, 0, :].rearrange(
                        "p (t d) -> p t d", t=2), ACT.Copy).then_inc(tcopied, 1)

        @block.vector
        def _(dve):
            own = Own(dve, own_v)
            V = nc.vector
            dve.wait_ge(ld, 16)
            xc, n_f, rem, poly, two_n = (tmp[:, n] for n in (2, 3, 4, 5, 6))
            V.memset(q[:, 0, 0], 1.0)
            V.memset(q[:, 1, 0], 0.0)
            own(V.tensor_scalar(xc, prm[:, 0], -87.0, 88.0, ALU.max, ALU.min))
            own(V.tensor_scalar(n_f, xc, 1.0 / math.log(2.0), None, ALU.mult))
            own(V.tensor_copy(n_i[:], n_f))
            own(V.tensor_copy(n_f, n_i[:]))
            V.tensor_scalar(two_n, n_f, 127.0, 8388608.0, ALU.add, ALU.mult)
            own(V.scalar_tensor_tensor(rem, n_f, -LN2_HIGH, xc, ALU.mult, ALU.add))
            own(V.scalar_tensor_tensor(rem, n_f, -LN2_LOW, rem, ALU.mult, ALU.add))
            V.tensor_copy(n_i[:], two_n)
            own(V.tensor_scalar(poly, rem, 1.0 / math.factorial(7), None, ALU.mult))
            for k in range(6, 0, -1):
                own(V.scalar_tensor_tensor(poly, poly, 1.0 / math.factorial(k), rem, ALU.add, ALU.mult))
            own(V.scalar_tensor_tensor(tmp[:, 0], poly, 1.0, n_i[:].bitcast(F32), ALU.add, ALU.mult))
            dve.wait_ge(ex, 1)

            def operands(z):
                zs = slice(z * HZ, (z + 1) * HZ)
                dt, er, a, b, am, bb, den, nr, rr, ii = (tmp[:, n, zs] for n in range(10))
                V.scalar_tensor_tensor(a, er, -0.5, dt, ALU.mult, ALU.mult)
                own(V.scalar_tensor_tensor(b, prm[:, 2, zs], 0.5, dt, ALU.mult, ALU.mult))
                V.tensor_scalar(am, a, -1.0, 1.0, ALU.mult, ALU.add)
                V.tensor_tensor(bb, b, b, ALU.mult)
                own(V.tensor_tensor(nr, a, a, ALU.mult))
                V.tensor_tensor(den, am, am, ALU.mult)
                own(V.tensor_tensor(nr, nr, bb, ALU.add))
                V.tensor_tensor(den, den, bb, ALU.add)
                own(V.tensor_scalar(nr, nr, -1.0, 1.0, ALU.mult, ALU.add))
                own(V.reciprocal(den, den))
                V.tensor_tensor(pw[:, 0, 0, zs], nr, den, ALU.mult)
                own(V.scalar_tensor_tensor(pw[:, 0, 1, zs], b, 2.0, den, ALU.mult, ALU.mult))
                for k in range(6):
                    r, i = pw[:, k, 0, zs], pw[:, k, 1, zs]
                    V.tensor_tensor(rr, r, r, ALU.mult)
                    V.scalar_tensor_tensor(pw[:, k + 1, 1, zs], r, 2.0, i, ALU.mult, ALU.mult)
                    own(V.tensor_tensor(ii, i, i, ALU.mult))
                    own(V.tensor_tensor(pw[:, k + 1, 0, zs], rr, ii, ALU.subtract))
                V.tensor_copy(q[:, 0, 1, zs], pw[:, 0, 0, zs])
                own(V.tensor_copy(q[:, 1, 1, zs], pw[:, 0, 1, zs]))
                dve.sem_inc(pwr, 1)
                for k in range(1, levels):
                    n = 1 << k
                    if k > 1:
                        dve.wait_ge(qim, z * (levels - 1) + k - 1)
                    pr = pw[:, k, 0, zs].unsqueeze(1).to_broadcast([P, n, HZ])
                    pi = pw[:, k, 1, zs].unsqueeze(1).to_broadcast([P, n, HZ])
                    V.tensor_tensor(q[:, 0, n:2 * n, zs], q[:, 0, 0:n, zs], pr, ALU.mult)
                    own(V.tensor_tensor(qt[:, 0, 0:n], q[:, 1, 0:n, zs], pi, ALU.mult))
                    V.tensor_tensor(q[:, 0, n:2 * n, zs], q[:, 0, n:2 * n, zs], qt[:, 0, 0:n], ALU.subtract).then_inc(qre, 1)
                    dve.wait_ge(qre, z * (levels - 1) + k)
                if z == 0:
                    dve.wait_ge(c_ld, 16)
                br = prm[:, 3, zs].unsqueeze(1).to_broadcast([P, B, HZ])
                bi = prm[:, 4, zs].unsqueeze(1).to_broadcast([P, B, HZ])
                t0, t1 = xt[:, 0, :, zs], xt[:, 1, :, zs]
                cr, ci, re, nim = cin[:, 0, :, zs], cin[:, 1, :, zs], x[:, 0, 0, :, zs], x[:, 1, 0, :, zs]
                V.scalar_tensor_tensor(re, cr, 2.0, br, ALU.mult, ALU.mult)
                own(V.scalar_tensor_tensor(t0, ci, 2.0, bi, ALU.mult, ALU.mult))
                V.scalar_tensor_tensor(t1, ci, -2.0, br, ALU.mult, ALU.mult)
                V.tensor_tensor(re, re, t0, ALU.subtract)
                own(V.scalar_tensor_tensor(nim, cr, -2.0, bi, ALU.mult, ALU.mult))
                own(V.tensor_tensor(nim, nim, t1, ALU.add))
                sr = pw[:, 6, 0, zs].unsqueeze(1).to_broadcast([P, B, HZ])
                si = pw[:, 6, 1, zs].unsqueeze(1).to_broadcast([P, B, HZ])
                for a_ in range(1, NA):
                    cr, cn = x[:, 0, a_ - 1, :, zs], x[:, 1, a_ - 1, :, zs]
                    re, nim = x[:, 0, a_, :, zs], x[:, 1, a_, :, zs]
                    V.tensor_tensor(re, cr, sr, ALU.mult)
                    own(V.tensor_tensor(t0, cn, si, ALU.mult))
                    V.tensor_tensor(t1, cn, sr, ALU.mult)
                    V.tensor_tensor(re, re, t0, ALU.add)
                    own(V.tensor_tensor(nim, cr, si, ALU.mult))
                    own(V.tensor_tensor(nim, t1, nim, ALU.subtract))
                dve.sem_inc(xdone, 1)

            for z in range(2):
                operands(z)
            dve.wait_ge(cl, 16)
            hv = hT[:].rearrange("p k (c s) -> p k c s", c=B)
            V.tensor_copy(hv[:, :, :, 0], cls[:].unsqueeze(2).to_broadcast([NB, NA, B]))
            V.memset(hv[:, :, :, S], 0.0).then_inc(edge, 1)
            for g in range(first, len(groups), 2):
                dve.wait_ge(kdone, g + 1)
                copy_sums(V.tensor_copy, g).then_inc(kcopied_v, 1)
            for g in range(12):
                if g % 2 == 0:
                    dve.wait_ge(tdone, g + 1)
                    V.tensor_copy(h[:, 2 * g:2 * g + 2, :], pt[g % 4][0:TS, 0, :].rearrange(
                        "p (t d) -> p t d", t=2)).then_inc(hdone, 1)

        @block.gpsimd
        def _(pool):
            G = nc.gpsimd
            own = Own(pool, own_p)
            for z in range(2):
                zs = slice(z * HZ, (z + 1) * HZ)
                pool.wait_ge(pwr, z + 1)
                for k in range(1, levels):
                    n = 1 << k
                    if k > 1:
                        pool.wait_ge(qre, z * (levels - 1) + k - 1)
                    pr = pw[:, k, 0, zs].unsqueeze(1).to_broadcast([P, n, HZ])
                    pi = pw[:, k, 1, zs].unsqueeze(1).to_broadcast([P, n, HZ])
                    G.tensor_tensor(q[:, 1, n:2 * n, zs], q[:, 0, 0:n, zs], pi, ALU.mult)
                    own(G.tensor_tensor(qt[:, 1, 0:n], q[:, 1, 0:n, zs], pr, ALU.mult))
                    G.tensor_tensor(q[:, 1, n:2 * n, zs], q[:, 1, n:2 * n, zs], qt[:, 1, 0:n], ALU.add).then_inc(qim, 1)
                    pool.wait_ge(qim, z * (levels - 1) + k)

        @block.tensor
        def _(pe):
            for g, (z, half, h0) in enumerate(groups):
                if g % first == 0:
                    pe.wait_ge(xdone, z + 1)
                    pe.wait_ge(qre, (z + 1) * (levels - 1))
                    pe.wait_ge(qim, (z + 1) * (levels - 1))
                rows = slice(STATES * half, STATES * (half + 1))
                if g >= 4:
                    pe.wait_ge(*copied(g - 4))
                for hl in range(GC):
                    for part in range(2):
                        last = nc.tensor.matmul(ps[g % 4][0:NB, 0, NA * B * hl:NA * B * (hl + 1)],
                                                q[rows, part, :, h0 + hl], x[rows, part, :, :, h0 + hl],
                                                start=part == 0, stop=part == 1)
                last.then_inc(kdone, 1)
            pe.wait_ge(*copied(len(groups) - 2))
            pe.wait_ge(*copied(len(groups) - 1))
            pe.wait_ge(edge, 1)
            for g in range(12):
                if g >= 4:
                    pe.wait_ge(hdone if g % 2 == 0 else tcopied, (g - 4) // 2 + 1)
                for t in range(2):
                    for a_ in range(NA):
                        last = nc.tensor.transpose(pt[g % 4][0:TS, 0, t * D + a_ * NB:t * D + (a_ + 1) * NB],
                                                   hT[:, a_, (2 * g + t) * TS:(2 * g + t + 1) * TS], ident[0:NB, 0:NB])
                last.then_inc(tdone, 1)


class Norm:

    def __init__(self, ph):
        self.st = ph.sb("ln_st", [TS, NT, 6])
        self.t = ph.sb("ln_t", [TS, 6, NT])
        self.var_ready, self.std_ready = ph.sem("var_ready"), ph.sem("std_ready")

    def statistics(self, nc, dve, own, h):
        V, st = nc.vector, self.st
        s, d, v, qd, var, rstd = (self.t[:, n] for n in range(6))
        for t in range(NT):
            last = V.bn_stats(st[:, t], h[:, t, :])
        own(last)
        V.tensor_tensor(s, st[:, :, 1], st[:, :, 4], ALU.add)
        V.tensor_tensor(d, st[:, :, 1], st[:, :, 4], ALU.subtract)
        own(V.tensor_tensor(v, st[:, :, 2], st[:, :, 5], ALU.add))
        V.tensor_scalar(s, s, 0.5, None, ALU.mult)
        V.tensor_scalar(v, v, 1.0 / D, EPS, ALU.mult, ALU.add)
        own(V.scalar_tensor_tensor(qd, d, 0.25, d, ALU.mult, ALU.mult))
        V.tensor_tensor(var, v, qd, ALU.add).then_inc(self.var_ready, 1)
        dve.wait_ge(self.std_ready, 1)
        own(V.reciprocal(rstd, rstd))

    def root(self, nc, act):
        act.wait_ge(self.var_ready, 1)
        nc.scalar.activation(self.t[:, 5], self.t[:, 4], ACT.Sqrt).then_inc(self.std_ready, 1)

    def scale(self, nc, b, h, xn):
        for u in range(IT):
            t = b * IT + u
            last = nc.vector.tensor_scalar(xn[:, u, :], h[:, t, :], self.t[:, 0, bass.ds(t, 1)], self.t[:, 5, bass.ds(t, 1)],
                                           ALU.subtract, ALU.mult)
        return last


class ImageNorm:

    OWN = 4

    def __init__(self, ph):
        self.st = [ph.sb(f"ln_st{q}", [TS, IT, 6]) for q in range(2)]
        self.t = [ph.sb(f"ln_t{q}", [TS, 6, IT]) for q in range(2)]
        self.var_ready, self.std_ready = ph.sem("var_ready"), ph.sem("std_ready")

    def normalise(self, nc, dve, own, b, q, h, xn):
        V, st = nc.vector, self.st[q]
        s, d, v, qd, var, rstd = (self.t[q][:, n] for n in range(6))
        for u in range(IT):
            last = V.bn_stats(st[:, u], h[:, b * IT + u, :])
        own(last)
        V.tensor_tensor(s, st[:, :, 1], st[:, :, 4], ALU.add)
        V.tensor_tensor(d, st[:, :, 1], st[:, :, 4], ALU.subtract)
        own(V.tensor_tensor(v, st[:, :, 2], st[:, :, 5], ALU.add))
        V.tensor_scalar(s, s, 0.5, None, ALU.mult)
        V.tensor_scalar(v, v, 1.0 / D, EPS, ALU.mult, ALU.add)
        own(V.scalar_tensor_tensor(qd, d, 0.25, d, ALU.mult, ALU.mult))
        V.tensor_tensor(var, v, qd, ALU.add).then_inc(self.var_ready, 1)
        dve.wait_ge(self.std_ready, b + 1)
        own(V.reciprocal(rstd, rstd))
        for u in range(IT):
            last = V.tensor_scalar(xn[:, u, :], h[:, b * IT + u, :], s[:, u:u + 1], rstd[:, u:u + 1],
                                   ALU.subtract, ALU.mult)
        return last

    def root(self, nc, act, b, q):
        act.wait_ge(self.var_ready, b + 1)
        nc.scalar.activation(self.t[q][:, 5], self.t[q][:, 4], ACT.Sqrt).then_inc(self.std_ready, 1)


def pairs(loop, step):
    for q in range(2):
        step(q, q, False)
    with loop as i:
        for q in range(2):
            step(2 * i + q, q, False)
    for q in range(2):
        step(B - 2 + q, q, q == 1)


def transpose_image(nc, pt, xn, ident):
    for c in range(KC):
        for u in range(IT):
            last = nc.tensor.transpose(pt[:, c, u * TS:(u + 1) * TS], xn[:, u, c * P:(c + 1) * P], ident[0:TS, 0:TS])
    return last


def attention0_phase(nc, h, ident, A):
    GAMMA = 1.0 / 16.0
    with Phase(nc, "a0") as ph:
        sb, sem = ph.sb, ph.sem
        w = sb("w", [P, 3, KC, D])
        xn, xT = [sb(f"xn{q}", [TS, IT, D]) for q in range(2)], [sb(f"xT{q}", [P, KC, SP]) for q in range(2)]
        qk, v = [sb(f"qk{q}", [P, 2, KC, SP]) for q in range(2)], [sb(f"v{q}", [TS, IT, D]) for q in range(2)]
        pr, prT = sb("pr", [TS, IT, SP]), sb("prT", [TS, IT, IT, TS])
        mask = sb("mask", [TS, TS])
        sc = sb("sc", [TS, IT, SP])
        mx, nb, sm, rs = (sb(n, [TS, IT]) for n in ("mx", "nb", "sm", "rs"))
        norm = Norm(ph)
        pt, pq, pp = ph.ps("pt", 2), ph.ps("pq", 2), ph.ps("pp")
        pss = [ph.ps(f"pss{n}") for n in range(IT)]
        w_in, own_v, xn_ready, xt_ps, xt_ready = (sem(n) for n in ("w_in", "own_v", "xn_ready", "xt_ps", "xt_ready"))
        qk_ps, qk_ready, v_ps, v_ready, s_ps, nb_ready, p_ready = (sem(n) for n in (
            "qk_ps", "qk_ready", "v_ps", "v_ready", "s_ps", "nb_ready", "p_ready"))
        pt_ps, pt_ready, y_ps, y_done, mask_ready, mask_zero = (sem(n) for n in (
            "pt_ps", "pt_ready", "y_ps", "y_done", "mask_ready", "mask_zero"))
        block = ph.block()

        @block.sync
        def _(sp):
            sp.dma_start(w[:], A["a0_w"]).then_inc(w_in, 16)

        @block.gpsimd
        def _(pool):
            nc.gpsimd.memset(mask[:], 0.0).then_inc(mask_zero, 1)
            pool.wait_ge(mask_zero, 1)
            nc.gpsimd.affine_select(out=mask[:], in_=mask[:], compare_op=ALU.is_ge, fill=-1e30, base=0,
                                    pattern=[[-1, TS]], channel_multiplier=1).then_inc(mask_ready, 1)

        @block.vector
        def _(dve):
            V = nc.vector
            own = Own(dve, own_v)
            dve.wait_ge(mask_ready, 1)

            def queries(b, q):
                for f in range(KC):
                    dve.wait_ge(qk_ps, b * 4 + 2 * f + 1)
                    V.tensor_copy(qk[q][:, 0, f], pq[:, 0, 0:SP]).then_inc(qk_ready, 1)

            def step(b, q, last):
                for u in range(IT):
                    n = (u + 1) * TS
                    dve.wait_ge(s_ps, b * IT + u + 1)
                    if u:
                        V.tensor_copy(sc[:, u, 0:n - TS], pss[u][0:TS, 0, 0:n - TS])
                    own(V.tensor_tensor(sc[:, u, n - TS:n], pss[u][0:TS, 0, n - TS:n], mask[:], ALU.add))
                    own(V.tensor_reduce(mx[:, u:u + 1], sc[:, u, 0:n], AX.X, ALU.max))
                    V.tensor_scalar(nb[:, u:u + 1], mx[:, u:u + 1], -GAMMA, None, ALU.mult).then_inc(nb_ready, 1)
                if not last:
                    queries(b + 1, 1 - q)
                if not isinstance(b, int) or b + 2 < B:
                    norm.scale(nc, b + 2, h, xn[q]).then_inc(xn_ready, 1)
                for u in range(IT):
                    dve.wait_ge(y_ps, b * IT + u + 1)
                    own(V.reciprocal(rs[:, u:u + 1], sm[:, u:u + 1]))
                    V.scalar_tensor_tensor(h[:, b * IT + u, :], pss[u][0:TS, 0, 0:D], rs[:, u:u + 1],
                                           h[:, b * IT + u, :], ALU.mult, ALU.add).then_inc(y_done, 1)

            norm.statistics(nc, dve, own, h)
            norm.scale(nc, 0, h, xn[0]).then_inc(xn_ready, 1)
            norm.scale(nc, 1, h, xn[1]).then_inc(xn_ready, 1)
            queries(0, 0)
            pairs(own.loop(B // 2 - 2, 6 * IT, first=1), step)
            dve.wait_ge(y_done, B * IT)

        @block.scalar
        def _(act):
            A_ = nc.scalar.activation

            def copy_x(b, q):
                act.wait_ge(xt_ps, b + 1)
                A_(xT[q][:], pt[:, :, 0:SP], ACT.Copy).then_inc(xt_ready, 1)

            def keys_values(b, q):
                for f in range(KC):
                    if f == 1:
                        act.wait_ge(v_ps, b + 1)
                        A_(v[q][:, 0:2, :], pt[0:TS, 0, :].rearrange("p (t d) -> p t d", t=2), ACT.Copy)
                        A_(v[q][:, 2, :], pt[0:TS, 1, 0:D], ACT.Copy).then_inc(v_ready, 1)
                    act.wait_ge(qk_ps, b * 4 + 2 * f + 2)
                    A_(qk[q][:, 1, f], pq[:, 1, 0:SP], ACT.Copy).then_inc(qk_ready, 1)

            def step(b, q, last):
                if not last:
                    copy_x(b + 1, 1 - q)
                for u in range(IT):
                    n = (u + 1) * TS
                    act.wait_ge(nb_ready, b * IT + u + 1)
                    A_(pr[:, u, 0:n], sc[:, u, 0:n], ACT.Exp, bias=nb[:, u:u + 1], scale=GAMMA,
                       accum_out=sm[:, u:u + 1]).then_inc(p_ready, 1)
                if not last:
                    keys_values(b + 1, 1 - q)
                for u in range(IT):
                    act.wait_ge(pt_ps, b * IT + u + 1)
                    A_(prT[:, u, 0:u + 1, :], pp[0:TS, 0, 0:(u + 1) * TS].rearrange("p (j i) -> p j i", i=TS),
                       ACT.Copy).then_inc(pt_ready, 1)

            norm.root(nc, act)
            copy_x(0, 0)
            keys_values(0, 0)
            pairs(act.Fori(1, B // 2 - 1), step)

        @block.tensor
        def _(pe):
            pe.wait_ge(w_in, 16)

            def transposes(b, q):
                pe.wait_ge(xn_ready, b + 1)
                free(pe, v_ready, b)
                transpose_image(nc, pt, xn[q], ident).then_inc(xt_ps, 1)

            def projections(b, q):
                pe.wait_ge(xt_ready, b + 1)
                for f in range(KC):
                    if f == 1:
                        for u in range(IT):
                            for c in range(KC):
                                last = nc.tensor.matmul(pt[0:TS, u // 2, (u % 2) * D:(u % 2 + 1) * D],
                                                        xT[q][:, c, u * TS:(u + 1) * TS], w[:, 2, c, :],
                                                        start=c == 0, stop=c == KC - 1)
                        last.then_inc(v_ps, 1)
                    for m in range(2):
                        free(pe, qk_ready, b * 4 + 2 * f)
                        for c in range(KC):
                            last = nc.tensor.matmul(pq[:, m, 0:SP], w[:, m, c, f * P:(f + 1) * P], xT[q][:, c, :],
                                                    start=c == 0, stop=c == KC - 1)
                        last.then_inc(qk_ps, 1)

            def step(b, q, last_image):
                if not last_image:
                    transposes(b + 1, 1 - q)
                pe.wait_ge(qk_ready, b * 4 + 4)
                for u in range(IT):
                    n = (u + 1) * TS
                    free(pe, y_done, b * IT + u - 2)
                    for c in range(KC):
                        last = nc.tensor.matmul(pss[u][0:TS, 0, 0:n], qk[q][:, 0, c, u * TS:n], qk[q][:, 1, c, 0:n],
                                                start=c == 0, stop=c == KC - 1)
                    last.then_inc(s_ps, 1)
                pe.wait_ge(v_ready, b + 1)
                if not last_image:
                    projections(b + 1, 1 - q)
                for u in range(IT):
                    pe.wait_ge(p_ready, b * IT + u + 1)
                    free(pe, pt_ready, b * IT + u)
                    for j in range(u + 1):
                        last = nc.tensor.transpose(pp[0:TS, 0, j * TS:(j + 1) * TS], pr[:, u, j * TS:(j + 1) * TS],
                                                   ident[0:TS, 0:TS])
                    last.then_inc(pt_ps, 1)
                    pe.wait_ge(pt_ready, b * IT + u + 1)
                    for j in range(u + 1):
                        last = nc.tensor.matmul(pss[u][0:TS, 0, 0:D], prT[:, u, j, :], v[q][:, j, :],
                                                start=j == 0, stop=j == u)
                    last.then_inc(y_ps, 1)

            transposes(0, 0)
            projections(0, 0)
            pairs(pe.Fori(1, B // 2 - 1), step)


class Moe:

    def __init__(self, nc, A, n, experts, picks):
        self.n, self.E, self.K = n, experts, picks
        self.first = n == 0
        self.C = experts + (1 if self.first else 0)
        self.M = expert_tiles(experts, picks)
        self.rounds = -(-NT * TS * picks // P)
        self.A = {k[3:]: v for k, v in A.items() if k.startswith(f"m{n}_")}
        self.rows = nc.dram_tensor(f"moe{n}_rows", (NT, TS, D), F32).ap()
        self.ids = nc.dram_tensor(f"moe{n}_ids", (self.M * ETILE + P, 1), U32).ap()
        self.slots = nc.dram_tensor(f"moe{n}_slots", (self.rounds * P,), U32).ap()
        self.y = nc.dram_tensor(f"moe{n}_y", (self.M * ETILE, D), F32).ap()


def moe0_input_phase(nc, h, ident, m, lg):
    FC = FS // P
    E = m.E
    with Phase(nc, "mi0") as ph:
        sb, sem = ph.sb, ph.sem
        xn, xT = [sb(f"xn{q}", [TS, IT, D]) for q in range(2)], [sb(f"xT{q}", [P, KC, SP]) for q in range(2)]
        gw = sb("gw", [P, KC, E])
        w1, w2 = sb("w1", [P, KC, 2 * FS]), sb("w2", [P, FC, D])
        cols = sb("cols", [P, 3, FC])
        gl, mid = sb("gl", [P, FC, SP]), sb("mid", [P, FC, SP])
        norm = Norm(ph)
        pt, plog, pg, px = ph.ps("pt", 2), ph.ps("plog"), ph.ps("pg"), ph.ps("px")
        py = [ph.ps("py0"), ph.ps("py1")]
        w_in, own_v, xn_ready, xt_ps, xt_ready, lg_ps, lg_out = (sem(n) for n in (
            "w_in", "own_v", "xn_ready", "xt_ps", "xt_ready", "lg_ps", "lg_out"))
        g_ps, x_ps, g_ready, mid_ready, y_ps, y_done = (sem(n) for n in (
            "g_ps", "x_ps", "g_ready", "mid_ready", "y_ps", "y_done"))
        stored = [sem(f"stored{q}") for q in range(2)]
        block = ph.block()

        @block.sync
        def _(sp):
            for dst, name in ((gw, "gate"), (w1, "s_w1"), (w2, "s_w2"), (cols, "s_cols")):
                sp.dma_start(dst[:], m.A[name]).then_inc(w_in, 16)
            with sp.Fori(0, B // 2) as i:
                for q in range(2):
                    b = 2 * i + q
                    sp.wait_ge(xn_ready, b + 1)
                    sp.dma_start(m.rows[bass.ds(b * IT, IT)].rearrange("t p d -> p t d"), xn[q][:]).then_inc(stored[q], 16)
            for q in range(2):
                sp.wait_ge(stored[q], 16 * (B // 2))

        @block.vector
        def _(dve):
            V = nc.vector
            own = Own(dve, own_v)
            norm.statistics(nc, dve, own, h)
            norm.scale(nc, 0, h, xn[0]).then_inc(xn_ready, 1)
            dve.wait_ge(w_in, 16 * 4)
            for f in range(FC):
                last = V.tensor_scalar(w2[:, f, :], w2[:, f, :], cols[:, 2, f:f + 1], None, ALU.mult)
            own(last)
            dve.sem_inc(w_in, 1)

            def step(b, q, last_image):
                if not last_image:
                    free(dve, xt_ps, b)
                    if q:
                        dve.wait_ge(stored[0], b * 8 + 8)
                    else:
                        free(dve, stored[1], b * 8)
                    norm.scale(nc, b + 1, h, xn[1 - q]).then_inc(xn_ready, 1)
                for f in range(FC):
                    dve.wait_ge(g_ready, b * FC + f + 1)
                    dve.wait_ge(x_ps, b * FC + f + 1)
                    V.scalar_tensor_tensor(mid[:, f], px[:, 0, 0:SP], cols[:, 0, f:f + 1], gl[:, f],
                                           ALU.add, ALU.mult).then_inc(mid_ready, 1)
                dve.wait_ge(lg_ps, b + 1)
                V.tensor_copy(lg[:, bass.ds(b * IT, IT), :], plog[0:TS, 0, 0:IT * E].rearrange(
                    "p (t e) -> p t e", t=IT)).then_inc(lg_out, 1)
                for u in range(IT):
                    dve.wait_ge(y_ps, b * IT + u + 1)
                    V.tensor_tensor(h[:, b * IT + u, :], py[u % 2][0:TS, 0, 0:D], h[:, b * IT + u, :],
                                    ALU.add).then_inc(y_done, 1)

            pairs(dve.Fori(1, B // 2 - 1), step)
            dve.wait_ge(y_done, B * IT)

        @block.scalar
        def _(act):
            def copy_x(b, q):
                act.wait_ge(xt_ps, b + 1)
                nc.scalar.activation(xT[q][:], pt[:, :, 0:SP], ACT.Copy).then_inc(xt_ready, 1)

            def step(b, q, last_image):
                for f in range(FC):
                    act.wait_ge(g_ps, b * FC + f + 1)
                    nc.scalar.activation(gl[:, f], pg[:, 0, 0:SP], ACT.Gelu, bias=cols[:, 1, f:f + 1]).then_inc(g_ready, 1)
                if not last_image:
                    copy_x(b + 1, 1 - q)

            norm.root(nc, act)
            act.wait_ge(w_in, 16 * 4)
            copy_x(0, 0)
            pairs(act.Fori(1, B // 2 - 1), step)

        @block.tensor
        def _(pe):
            def transposes(b, q):
                pe.wait_ge(xn_ready, b + 1)
                transpose_image(nc, pt, xn[q], ident).then_inc(xt_ps, 1)

            def step(b, q, last_image):
                pe.wait_ge(xt_ready, b + 1)
                for f in range(FC):
                    free(pe, g_ready, b * FC + f)
                    for c in range(KC):
                        last = nc.tensor.matmul(pg[:, 0, 0:SP], w1[:, c, FS + f * P:FS + f * P + P], xT[q][:, c, :],
                                                start=c == 0, stop=c == KC - 1)
                    last.then_inc(g_ps, 1)
                    free(pe, mid_ready, b * FC + f)
                    for c in range(KC):
                        last = nc.tensor.matmul(px[:, 0, 0:SP], w1[:, c, f * P:f * P + P], xT[q][:, c, :],
                                                start=c == 0, stop=c == KC - 1)
                    last.then_inc(x_ps, 1)
                if not last_image:
                    transposes(b + 1, 1 - q)
                free(pe, lg_out, b)
                for u in range(IT):
                    for c in range(KC):
                        last = nc.tensor.matmul(plog[0:TS, 0, u * E:(u + 1) * E], xT[q][:, c, u * TS:(u + 1) * TS],
                                                gw[:, c, :], start=c == 0, stop=c == KC - 1)
                last.then_inc(lg_ps, 1)
                pe.wait_ge(mid_ready, b * FC + FC)
                for u in range(IT):
                    free(pe, y_done, b * IT + u - (0, 2, 1)[u])
                    for f in range(FC):
                        last = nc.tensor.matmul(py[u % 2][0:TS, 0, 0:D], mid[:, f, u * TS:(u + 1) * TS], w2[:, f, :],
                                                start=f == 0, stop=f == FC - 1)
                    last.then_inc(y_ps, 1)

            transposes(0, 0)
            pe.wait_ge(w_in, 16 * 4 + 1)
            pairs(pe.Fori(1, B // 2 - 1), step)


def moe1_input_phase(nc, h, ident, m, lg):
    E = m.E
    with Phase(nc, "mi1") as ph:
        sb, sem = ph.sb, ph.sem
        xn = sb("xn", [TS, NT, D])
        tn, xT = [sb(f"tn{q}", [TS, IT, D]) for q in range(2)], [sb(f"xT{q}", [P, KC, SP]) for q in range(2)]
        gw, scale_row, gb = sb("gw", [P, KC, E]), sb("scale_row", [TS, D]), sb("gb", [TS, E])
        sq, ss, rr = sb("sq", [TS, IT, D]), sb("ss", [TS, NT]), sb("rr", [TS, 2, NT])
        norm = Norm(ph)
        pt, plog = [ph.ps(f"pt{q}", 2) for q in range(2)], [ph.ps(f"plog{q}") for q in range(2)]
        w_in, own_v, own_s, xn_ready, rows_ready, xt_ps, xt_ready, lg_ps, lg_out = (sem(n) for n in (
            "w_in", "own_v", "own_s", "xn_ready", "rows_ready", "xt_ps", "xt_ready", "lg_ps", "lg_out"))
        ms_ready, rms_ready, h_done = (sem(n) for n in ("ms_ready", "rms_ready", "h_done"))
        stored = [sem(f"stored{q}") for q in range(2)]
        block = ph.block()

        @block.sync
        def _(sp):
            for dst, src in ((gw, m.A["gate"]), (scale_row, m.A["scale"].to_broadcast([TS, D])),
                             (gb, m.A["gate_b"].to_broadcast([TS, E]))):
                sp.dma_start(dst[:], src).then_inc(w_in, 16)
            with sp.Fori(0, B // 2) as i:
                for q in range(2):
                    b = 2 * i + q
                    sp.wait_ge(rows_ready, b + 1)
                    sp.dma_start(m.rows[bass.ds(b * IT, IT)].rearrange("t p d -> p t d"), tn[q][:]).then_inc(stored[q], 16)
            for q in range(2):
                sp.wait_ge(stored[q], 16 * (B // 2))

        @block.gpsimd
        def _(pool):
            pool.wait_ge(xn_ready, B)
            nc.gpsimd.tensor_tensor(h[:], h[:], xn[:], ALU.add).then_inc(h_done, 1)
            pool.wait_ge(h_done, 1)

        @block.vector
        def _(dve):
            V = nc.vector
            own = Own(dve, own_v)
            norm.statistics(nc, dve, own, h)
            with dve.Fori(0, B) as b:
                norm.scale(nc, b, h, xn[:, bass.ds(b * IT, IT)]).then_inc(xn_ready, 1)
            dve.wait_ge(w_in, 16 * 3)
            dve.wait_ge(own_s, NT)
            V.tensor_scalar(rr[:, 0], ss[:], 1.0 / D, EPS, ALU.mult, ALU.add).then_inc(ms_ready, 1)
            dve.wait_ge(rms_ready, 1)
            own(V.reciprocal(rr[:, 1], rr[:, 1]))
            dve.wait_ge(xn_ready, B)

            def logits(b, q):
                dve.wait_ge(lg_ps, b + 1)
                V.tensor_tensor(lg[:, bass.ds(b * IT, IT), :], plog[q][0:TS, 0, 0:IT * E].rearrange("p (t e) -> p t e", t=IT),
                                gb[:].unsqueeze(1).to_broadcast([TS, IT, E]), ALU.add).then_inc(lg_out, 1)

            def step(b, q, last_image):
                free(dve, stored[q], b * 8 - 8 * q)
                free(dve, xt_ps, b - 1)
                for u in range(IT):
                    t = b * IT + u
                    last = V.scalar_tensor_tensor(tn[q][:, u, :], xn[:, t, :], rr[:, 1, bass.ds(t, 1)], scale_row[:],
                                                  ALU.mult, ALU.mult)
                last.then_inc(rows_ready, 1)
                if not isinstance(b, int) or b > 0:
                    logits(b - 1, 1 - q)

            pairs(dve.Fori(1, B // 2 - 1), step)
            logits(B - 1, 1)
            dve.wait_ge(lg_out, B)

        @block.scalar
        def _(act):
            norm.root(nc, act)
            with act.Fori(0, B) as b:
                act.wait_ge(xn_ready, b + 1)
                for u in range(IT):
                    t = b * IT + u
                    nc.scalar.activation(sq[:, u], xn[:, t, :], ACT.Square, accum_out=ss[:, bass.ds(t, 1)]).then_inc(own_s, 1)
                act.wait_ge(own_s, b * IT + IT)
            act.wait_ge(ms_ready, 1)
            nc.scalar.activation(rr[:, 1], rr[:, 0], ACT.Sqrt).then_inc(rms_ready, 1)

            def step(b, q, last_image):
                act.wait_ge(xt_ps, b + 1)
                free(act, lg_ps, b - 1)
                nc.scalar.activation(xT[q][:], pt[q][:, :, 0:SP], ACT.Copy).then_inc(xt_ready, 1)

            pairs(act.Fori(1, B // 2 - 1), step)

        @block.tensor
        def _(pe):
            pe.wait_ge(w_in, 16 * 3)

            def transposes(b, q):
                pe.wait_ge(rows_ready, b + 1)
                free(pe, xt_ready, b - 1)
                transpose_image(nc, pt[q], tn[q], ident).then_inc(xt_ps, 1)

            def step(b, q, last_image):
                if not last_image:
                    transposes(b + 1, 1 - q)
                pe.wait_ge(xt_ready, b + 1)
                free(pe, lg_out, b - 1)
                for u in range(IT):
                    for c in range(KC):
                        last = nc.tensor.matmul(plog[q][0:TS, 0, u * E:(u + 1) * E], xT[q][:, c, u * TS:(u + 1) * TS],
                                                gw[:, c, :], start=c == 0, stop=c == KC - 1)
                last.then_inc(lg_ps, 1)

            transposes(0, 0)
            pairs(pe.Fori(1, B // 2 - 1), step)


def routing_phase(nc, h, ident, m, lg, wts, gslot, te, idcols):
    E, K, M, C = m.E, m.K, m.M, m.C
    TB = BANK // E if NT * E > BANK else NT
    TB = max(n for n in range(1, TB + 1) if NT % n == 0)
    NB = NT // TB
    with Phase(nc, f"rt{m.n}") as ph:
        sb, sem = ph.sb, ph.sem
        work, tmp = sb("work", [TS, NT, E]), sb("tmp", [TS, NT, E])
        oh = sb("oh", [TS, K, NT, E])
        sel, top = sb("sel", [TS, NT]), sb("top", [TS, NT, K])
        ex, ssum = sb("ex", [TS, NT, K]), sb("ssum", [TS, 2, NT])
        mask, cum = sb("mask", [TS, NT, E]), [sb("cum0", [TS, NT, E]), sb("cum1", [TS, NT, E])]
        rank = sb("rank", [TS, NT, E])
        slot, comb = sb("slot", [TS, NT, K]), sb("comb", [TS, NT, C])
        combT, b2 = sb("combT", [C, NTOK]), sb("b2", [C, D])
        e5 = sb("e5", [TS, 5, E])
        ti = sb("ti", [TS, E], I32)
        tef, cmp = sb("tef", [1, M]), sb("cmp", [1, M, E])
        desc, real, padslot = sb("desc", [TS, E]), sb("real", [TS, NT]), sb("padslot", [TS, NT, K])
        iot = sb("iot", [1, M])
        tri, ones = sb("tri", [TS, TS]), sb("ones", [TS, TS])
        sslot = sb("sslot", [TS, NT, K], U32)
        tok, slot_cols = sb("tok", [P, m.rounds], U32), sb("slot_cols", [P, m.rounds], U32)
        zero = sb("zero", [P, M + 1], U32)
        pr = ph.ps("pr", NB)
        pc = ph.ps("pc")
        pt2 = [ph.ps("pt0"), ph.ps("pt1")]
        pb = [ph.ps("pb0"), ph.ps("pb1")]
        c_in, own_v, lg_shift, ex_ready = (sem(n) for n in ("c_in", "own_v", "lg_shift", "ex_ready"))
        mask_ready, rank_ps, slots_ready, zeroed, cleared, sent, ids_in = (sem(n) for n in (
            "mask_ready", "rank_ps", "slots_ready", "zeroed", "cleared", "sent", "ids_in"))
        comb_ready, ct_ps, ct_ready, b_ps, b_done = (sem(n) for n in ("comb_ready", "ct_ps", "ct_ready", "b_ps", "b_done"))
        slots_out, pairs_in = sem("slots_out"), sem("pairs_in")
        block = ph.block()

        def per_tile(v):
            return v.unsqueeze(1).to_broadcast([TS, NT, E])

        def per_expert(v):
            return v.unsqueeze(2).to_broadcast([TS, NT, E])

        @block.sync
        def _(sp):
            for dst, name in ((desc, "desc"), (real, "real"), (padslot, "padslot"), (iot, "tile_no"), (tri, "tri"),
                              (tok, "tok"), (b2, "b2")):
                sp.dma_start(dst[:], m.A[name]).then_inc(c_in, 16)
            sp.wait_ge(zeroed, 1)
            sp.dma_start(m.ids.rearrange("(p n) o -> p (n o)", p=P), zero[:]).then_inc(cleared, 16)
            n = TS * NT * K
            sp.dma_start(m.slots[n:].unsqueeze(0), m.A["tail"]).then_inc(slots_out, 16)
            sp.wait_ge(slots_ready, 1)
            sp.dma_start(m.slots[0:n].rearrange("(p n) -> p n", p=TS), sslot[:].rearrange("p t k -> p (t k)")).then_inc(slots_out, 16)
            sp.wait_ge(slots_out, 32)
            sp.dma_start(slot_cols[:], m.slots.rearrange("(p n) -> p n", p=P)).then_inc(pairs_in, 16)
            sp.wait_ge(cleared, 16)
            sp.wait_ge(sent, 16 * m.rounds)
            sp.dma_start(idcols[:], m.ids[0:M * ETILE].rearrange("(t p) o -> p (t o)", p=ETILE),
                         allow_slow_non_contiguous=True).then_inc(ids_in, 16)
            sp.wait_ge(ids_in, 16)

        @block.gpsimd
        def _(pool):
            G = nc.gpsimd
            G.memset(zero[:], 0).then_inc(zeroed, 1)
            G.memset(ones[:], 1.0).then_inc(zeroed, 1)
            pool.wait_ge(cleared, 16)
            pool.wait_ge(pairs_in, 16)
            for n in range(m.rounds):
                G.indirect_dma_start(m.ids, bass.IndirectOffsetOnAxis(slot_cols[:, n:n + 1], 0),
                                     tok[:, n:n + 1], None).then_inc(sent, 16)
            pool.wait_ge(sent, 16 * m.rounds)

        @block.vector
        def _(dve):
            V = nc.vector
            own = Own(dve, own_v)
            dve.wait_ge(c_in, 16 * 7)
            for k in range(K):
                left = work if k else lg
                own(V.tensor_reduce(top[:, :, k], left[:], AX.X, ALU.max))
                own(V.tensor_tensor(tmp[:], left[:], per_expert(top[:, :, k]), ALU.is_equal))
                own(V.tensor_tensor(tmp[:], tmp[:], per_tile(desc[:]), ALU.mult))
                own(V.tensor_reduce(sel[:], tmp[:], AX.X, ALU.max))
                own(V.tensor_tensor(oh[:, k], per_tile(desc[:]), per_expert(sel[:]), ALU.is_equal))
                if k < K - 1:
                    own(V.scalar_tensor_tensor(work[:], oh[:, k], -3e38, left[:], ALU.mult, ALU.add))
            own(V.tensor_tensor(mask[:], oh[:, 0], oh[:, 1], ALU.add))
            for k in range(2, K):
                own(V.tensor_tensor(mask[:], mask[:], oh[:, k], ALU.add))
            own(V.tensor_tensor(mask[:], mask[:], per_expert(real[:]), ALU.mult))
            src, n, step = mask, 0, 1
            while step < NT:
                dst = cum[n % 2]
                V.tensor_copy(dst[:, 0:step], src[:, 0:step])
                own(V.tensor_tensor(dst[:, step:], src[:, step:], src[:, 0:NT - step], ALU.add))
                src, n, step = dst, n + 1, 2 * step
            assert src is cum[0]
            dve.sem_inc(mask_ready, 1)
            dve.wait_ge(rank_ps, 1)
            cnt, tiles, ones_row, end, base = (e5[:, n] for n in range(5))
            own(V.tensor_scalar(cnt, pc[0:TS, 0, 0:E], float(ETILE - 1), 1.0 / ETILE, ALU.add, ALU.mult))
            V.memset(ones_row, 1.0)
            own(V.tensor_scalar(cnt, cnt, 0.5 / ETILE - 0.5, None, ALU.add))
            own(V.tensor_copy(ti[:], cnt))
            own(V.tensor_copy(tiles, ti[:]))
            own(V.tensor_tensor_scan(end, ones_row, tiles, 0.0, ALU.mult, ALU.add))
            own(V.tensor_tensor(base, end, tiles, ALU.subtract))
            own(V.tensor_scalar(base, base, float(ETILE), None, ALU.mult))
            own(V.tensor_tensor(cmp[:], end[0:1].unsqueeze(1).to_broadcast([1, M, E]),
                                iot[:].unsqueeze(2).to_broadcast([1, M, E]), ALU.is_le))
            own(V.tensor_reduce(tef[:], cmp[:], AX.X, ALU.add))
            own(V.tensor_scalar(tef[:], tef[:], float(E - 1), None, ALU.min))
            own(V.tensor_copy(te[:], tef[:]))
            for n in range(NB):
                last = V.tensor_tensor(rank[:, n * TB:(n + 1) * TB], pr[0:TS, n, 0:TB * E].rearrange(
                    "p (t e) -> p t e", t=TB), base.unsqueeze(1).to_broadcast([TS, TB, E]), ALU.add)
            own(last)
            for k in range(K):
                own(V.tensor_tensor(tmp[:], rank[:], oh[:, k], ALU.mult))
                own(V.tensor_reduce(slot[:, :, k], tmp[:], AX.X, ALU.add))
            own(V.tensor_tensor(slot[:], slot[:], real[:].unsqueeze(2).to_broadcast([TS, NT, K]), ALU.mult))
            V.tensor_copy(gslot[:], slot[:])
            own(V.tensor_tensor(slot[:], slot[:], padslot[:], ALU.add))
            V.tensor_copy(sslot[:], slot[:]).then_inc(slots_ready, 1)
            V.tensor_tensor(ex[:], top[:], top[:, :, 0:1].to_broadcast([TS, NT, K]), ALU.subtract)
            V.tensor_tensor(work[:], lg[:], per_expert(top[:, :, 0]), ALU.subtract).then_inc(lg_shift, 1)
            dve.wait_ge(ex_ready, 1)
            if m.first:
                own(V.tensor_reduce(ssum[:, 0], work[:], AX.X, ALU.add))
                own(V.reciprocal(ssum[:, 0], ssum[:, 0]))
                own(V.tensor_tensor(ex[:], ex[:], ssum[:, 0].unsqueeze(2).to_broadcast([TS, NT, K]), ALU.mult))
                own(V.tensor_reduce(ssum[:, 1], ex[:], AX.X, ALU.add))
                own(V.tensor_scalar(ssum[:, 1], ssum[:, 1], 1e-20, None, ALU.add))
            else:
                own(V.tensor_reduce(ssum[:, 1], ex[:], AX.X, ALU.add))
            own(V.reciprocal(ssum[:, 1], ssum[:, 1]))
            own(V.tensor_tensor(wts[:], ex[:], ssum[:, 1].unsqueeze(2).to_broadcast([TS, NT, K]), ALU.mult))
            if C > E:
                V.memset(comb[:, :, E:C], 1.0)
            own(V.tensor_tensor(comb[:, :, 0:E], oh[:, 0], per_expert(wts[:, :, 0]), ALU.mult))
            for k in range(1, K):
                own(V.tensor_tensor(tmp[:], oh[:, k], per_expert(wts[:, :, k]), ALU.mult))
                own(V.tensor_tensor(comb[:, :, 0:E], comb[:, :, 0:E], tmp[:], ALU.add))
            dve.sem_inc(comb_ready, 1)
            for g in range(NT // 2):
                dve.wait_ge(b_ps, g + 1)
                V.tensor_tensor(h[:, 2 * g:2 * g + 2, :], pb[g % 2][0:TS, 0, :].rearrange("p (t d) -> p t d", t=2),
                                h[:, 2 * g:2 * g + 2, :], ALU.add).then_inc(b_done, 1)
            dve.wait_ge(b_done, NT // 2)

        @block.scalar
        def _(act):
            act.wait_ge(lg_shift, 1)
            if m.first:
                nc.scalar.activation(work[:], work[:], ACT.Exp)
            nc.scalar.activation(ex[:], ex[:], ACT.Exp).then_inc(ex_ready, 1)
            for g in range(NT // 4):
                act.wait_ge(ct_ps, g + 1)
                nc.scalar.activation(combT[:, g * 4 * TS:(g + 1) * 4 * TS], pt2[g % 2][0:C, 0, 0:4 * TS],
                                     ACT.Copy).then_inc(ct_ready, 1)

        @block.tensor
        def _(pe):
            pe.wait_ge(c_in, 16 * 7)
            pe.wait_ge(zeroed, 2)
            pe.wait_ge(mask_ready, 1)
            incl = cum[0]
            for n in range(NB):
                nc.tensor.matmul(pr[0:TS, n, 0:TB * E], tri[:], mask[:, n * TB:(n + 1) * TB].rearrange("p t e -> p (t e)"),
                                 start=True, stop=False)
                t0 = n * TB
                s = 1 if n == 0 else 0
                nc.tensor.matmul(pr[0:TS, n, s * E:TB * E], ones[:],
                                 incl[:, t0 + s - 1:t0 + TB - 1].rearrange("p t e -> p (t e)"), start=False, stop=True)
            nc.tensor.matmul(pc[0:TS, 0, 0:E], ones[:], incl[:, NT - 1], start=True, stop=True).then_inc(rank_ps, 1)
            pe.wait_ge(comb_ready, 1)
            for g in range(NT // 4):
                if g >= 2:
                    pe.wait_ge(ct_ready, g - 1)
                for t in range(4):
                    last = nc.tensor.transpose(pt2[g % 2][0:C, 0, t * TS:(t + 1) * TS], comb[:, 4 * g + t], ident[0:TS, 0:TS])
                last.then_inc(ct_ps, 1)
            pe.wait_ge(ct_ready, NT // 4)
            for g in range(NT // 2):
                if g >= 2:
                    pe.wait_ge(b_done, g - 1)
                for t in range(2):
                    last = nc.tensor.matmul(pb[g % 2][0:TS, 0, t * D:(t + 1) * D],
                                            combT[:, (2 * g + t) * TS:(2 * g + t + 1) * TS], b2[:], start=True, stop=True)
                last.then_inc(b_ps, 1)


def experts_phase(nc, ident, m, te, idcols):
    M, E = m.M, m.E
    R = 4
    NI = M // R
    WC = KC * 2 * F + KC * D + 6
    with Phase(nc, f"ex{m.n}") as ph:
        sb, sem = ph.sb, ph.sem
        w = [sb(f"w{r}", [P, WC]) for r in range(R)]
        idx = [sb(f"idx{r}", [ETILE, 1], U32) for r in range(R)]
        xg = [sb(f"xg{r}", [ETILE, D]) for r in range(R)]
        y = [sb(f"y{r}", [ETILE, D]) for r in range(R)]
        xT = [sb(f"xT{q}", [P, KC, ETILE]) for q in range(2)]
        g = [sb(f"g{q}", [P, KC, ETILE]) for q in range(2)]
        li = [sb(f"li{q}", [P, KC, ETILE]) for q in range(2)]
        mid = [sb(f"mid{q}", [P, KC, ETILE]) for q in range(2)]
        glu = [sb(f"glu{q}", [P, KC, ETILE]) for q in range(2)] if not m.first else None
        px, pg, pl, py = ([ph.ps(f"{n}{q}") for q in range(2)] for n in ("px", "pg", "pl", "py"))
        w_in, x_in, y_out = ([sem(f"{n}{r}") for r in range(R)] for n in ("w_in", "x_in", "y_out"))
        g_ps, l_ps, li_ready, idx_seen = (sem(n) for n in ("g_ps", "l_ps", "li_ready", "idx_seen"))
        idx_ready, xt_ps, xt_ready, g_ready, mid_ready, y_ps, y_ready, own_v = (sem(n) for n in (
            "idx_ready", "xt_ps", "xt_ready", "g_ready", "mid_ready", "y_ps", "y_ready", "own_v"))
        glu_ready = sem("glu_ready")
        block = ph.block()

        def up(r, c, f):
            return w[r][:, c * 2 * F + f * P:c * 2 * F + (f + 1) * P]

        def down(r, f):
            o = KC * 2 * F + f * D
            return w[r][:, o:o + D]

        def col(r, n):
            o = KC * 2 * F + KC * D + n
            return w[r][:, o:o + 1]

        @block.sync
        def _(sp):
            def load(i, r):
                t = R * i + r
                free(sp, y_ps, t - 3)
                e = sp.value_load(te[0:1, bass.ds(t, 1)], min_val=0, max_val=E - 1)
                sp.dma_start(w[r][:], m.A["w"][bass.ds(e, 1)].rearrange("o p n -> (o p) n")).then_inc(w_in[r], 16)

            def store(i, r):
                t = R * i + r
                sp.wait_ge(y_ready, t + 1)
                sp.dma_start(m.y[bass.ds(t * ETILE, ETILE)], y[r][:]).then_inc(y_out[r], 16)

            for r in range(R):
                load(0, r)
            with sp.Fori(1, NI) as i:
                for r in range(R):
                    load(i, r)
                    store(i - 1, r)
            for r in range(R):
                store(NI - 1, r)
                sp.wait_ge(y_out[r], 16 * NI)

        @block.gpsimd
        def _(pool):
            def gather(i, r):
                t = R * i + r
                free(pool, xt_ps, t - 3)
                nc.gpsimd.tensor_copy(idx[r][:], idcols[:, bass.ds(t, 1)]).then_inc(idx_ready, 1)
                pool.wait_ge(idx_ready, t + 1)
                pool.sem_inc(idx_seen, 1)
                nc.gpsimd.indirect_dma_start(xg[r][:], None, m.rows.rearrange("t p d -> (t p) d"),
                                             bass.IndirectOffsetOnAxis(idx[r][:], 0)).then_inc(x_in[r], 16)

            for r in range(R):
                gather(0, r)
            with pool.Fori(1, NI) as i:
                for r in range(R):
                    gather(i, r)
            for r in range(R):
                pool.wait_ge(x_in[r], 16 * NI)

        @block.tensor
        def _(pe):
            def transposes(i, r):
                t, q = R * i + r, r % 2
                pe.wait_ge(x_in[r], 16 * i + 16)
                free(pe, xt_ready, t - 1)
                for c in range(KC):
                    last = nc.tensor.transpose(px[q][:, 0, c * P:(c + 1) * P], xg[r][:, c * P:(c + 1) * P], ident[:])
                last.then_inc(xt_ps, 1)

            def up_products(i, r):
                t, q = R * i + r, r % 2
                pe.wait_ge(w_in[r], 16 * i + 16)
                pe.wait_ge(xt_ready, t + 1)
                free(pe, mid_ready, t - 1)
                for banks, f0, done in ((pg, KC, g_ps), (pl, 0, l_ps)):
                    for f in range(KC):
                        for c in range(KC):
                            last = nc.tensor.matmul(banks[q][:, 0, f * P:(f + 1) * P], up(r, c, f0 + f), xT[q][:, c],
                                                    start=c == 0, stop=c == KC - 1)
                    last.then_inc(done, 1)

            def down_products(i, r):
                t, q = R * i + r, r % 2
                pe.wait_ge(mid_ready, t + 1)
                free(pe, y_ready, t - 1)
                for f in range(KC):
                    last = nc.tensor.matmul(py[q][:, 0, 0:D], mid[q][:, f], down(r, f), start=f == 0, stop=f == KC - 1)
                last.then_inc(y_ps, 1)

            def four_tiles(i, first=False, last=False):
                for r in range(R):
                    if not (last and r == R - 1):
                        transposes(*((i, r + 1) if r < R - 1 else (i + 1, 0)))
                    up_products(i, r)
                    if not (first and r == 0):
                        down_products(*((i, r - 1) if r > 0 else (i - 1, R - 1)))

            transposes(0, 0)
            four_tiles(0, first=True)
            with pe.Fori(1, NI - 1) as i:
                four_tiles(i)
            four_tiles(NI - 1, last=True)
            down_products(NI - 1, R - 1)

        @block.scalar
        def _(act):
            A_ = nc.scalar.activation

            def copy_x(i, r):
                t, q = R * i + r, r % 2
                act.wait_ge(xt_ps, t + 1)
                A_(xT[q][:], px[q][:, 0, 0:D].rearrange("p (c t) -> p c t", c=KC), ACT.Copy).then_inc(xt_ready, 1)

            def gates(i, r):
                t, q = R * i + r, r % 2
                if m.first:
                    act.wait_ge(g_ps, t + 1)
                    for f in range(KC):
                        last = A_(g[q][:, f], pg[q][:, 0, f * P:(f + 1) * P], ACT.Gelu, bias=col(r, KC + f))
                else:
                    act.wait_ge(glu_ready, t + 1)
                    last = A_(g[q][:], glu[q][:], ACT.Gelu_apprx_sigmoid)
                last.then_inc(g_ready, 1)

            def copy_y(i, r):
                t, q = R * i + r, r % 2
                act.wait_ge(y_ps, t + 1)
                free(act, y_out[r], 16 * i)
                A_(y[r][:], py[q][:, 0, 0:D], ACT.Copy).then_inc(y_ready, 1)

            def four_tiles(i, first=False, last=False):
                for r in range(R):
                    if not (last and r == R - 1):
                        copy_x(*((i, r + 1) if r < R - 1 else (i + 1, 0)))
                    gates(i, r)
                    if not (first and r == 0):
                        copy_y(*((i, r - 1) if r > 0 else (i - 1, R - 1)))

            copy_x(0, 0)
            four_tiles(0, first=True)
            with act.Fori(1, NI - 1) as i:
                four_tiles(i)
            four_tiles(NI - 1, last=True)
            copy_y(NI - 1, R - 1)

        @block.vector
        def _(dve):
            V = nc.vector
            own = Own(dve, own_v)
            with own.loop(NI, R) as i:
                for r in range(R):
                    t, q = R * i + r, r % 2
                    if m.first:
                        dve.wait_ge(l_ps, t + 1)
                        for f in range(KC):
                            last = V.tensor_scalar(li[q][:, f], pl[q][:, 0, f * P:(f + 1) * P], col(r, f),
                                                   col(r, 2 * KC + f), ALU.add, ALU.mult)
                        own(last)
                        dve.wait_ge(g_ready, t + 1)
                        V.tensor_tensor(mid[q][:], li[q][:], g[q][:], ALU.mult).then_inc(mid_ready, 1)
                    else:
                        dve.wait_ge(g_ps, t + 1)
                        for f in range(KC):
                            last = V.tensor_scalar(glu[q][:, f], pg[q][:, 0, f * P:(f + 1) * P], col(r, KC + f),
                                                   LIMIT, ALU.add, ALU.min)
                        last.then_inc(glu_ready, 1)
                        dve.wait_ge(l_ps, t + 1)
                        for f in range(KC):
                            last = V.tensor_scalar(li[q][:, f], pl[q][:, 0, f * P:(f + 1) * P], col(r, f),
                                                   -LIMIT, ALU.add, ALU.max)
                        own(last)
                        V.tensor_scalar(li[q][:], li[q][:], LIMIT, 1.0, ALU.min, ALU.add).then_inc(li_ready, 1)
                        dve.wait_ge(li_ready, t + 1)
                        dve.wait_ge(g_ready, t + 1)
                        V.tensor_tensor(mid[q][:], li[q][:], g[q][:], ALU.mult).then_inc(mid_ready, 1)


class Combine:

    def __init__(self, nc, ph, m, wts, gslot):
        self.nc, self.m, self.K, self.wts, self.gslot = nc, m, m.K, wts, gslot
        self.R = 2 * IT
        self.yg = [ph.sb(f"yg{r}", [TS, self.K, D]) for r in range(self.R)]
        self.y_in = [ph.sem(f"y_in{r}") for r in range(self.R)]
        self.added = ph.sem("added")

    OWN = IT

    def gathers(self, pool):
        for t in range(NT):
            r = t % self.R
            if t >= self.R:
                pool.wait_ge(self.added, t - self.R + 1)
            for k in range(self.K):
                self.nc.gpsimd.indirect_dma_start(self.yg[r][:, k], None, self.m.y,
                                                  bass.IndirectOffsetOnAxis(self.gslot[:, t, k:k + 1], 0)
                                                  ).then_inc(self.y_in[r], 16)
        for r in range(self.R):
            pool.wait_ge(self.y_in[r], 16 * self.K * (B // 2))

    def add(self, dve, own, b, q, h):
        for u in range(IT):
            t, r = b * IT + u, q * IT + u
            dve.wait_ge(self.y_in[r], (b - q) * (8 * self.K) + 16 * self.K)
            for k in range(self.K):
                ins = self.nc.vector.scalar_tensor_tensor(h[:, t, :], self.yg[r][:, k], self.wts[:, t, k:k + 1], h[:, t, :],
                                                          ALU.mult, ALU.add)
                if k < self.K - 1:
                    own(ins)
                else:
                    ins.then_inc(self.added, 1)


def output_phase(nc, h, m, wts, gslot, out):
    with Phase(nc, "out") as ph:
        comb = Combine(nc, ph, m, wts, gslot)
        own_v, stored = ph.sem("own_v"), ph.sem("stored")
        block = ph.block()

        @block.gpsimd
        def _(pool):
            comb.gathers(pool)

        @block.vector
        def _(dve):
            own = Own(dve, own_v)
            with own.loop(B // 2, 2 * comb.OWN * (m.K - 1)) as i:
                for q in range(2):
                    comb.add(dve, own, 2 * i + q, q, h)

        @block.sync
        def _(sp):
            with sp.Fori(0, B) as b:
                sp.wait_ge(comb.added, b * IT + IT)
                for u in range(IT):
                    n = TS if u < IT - 1 else S - (IT - 1) * TS
                    sp.dma_start(out[bass.ds(b, 1), u * TS:u * TS + n, :].rearrange("o p d -> p (o d)"),
                                 h[0:n, b * IT + u, :]).then_inc(stored, 16)
            sp.wait_ge(stored, 16 * IT * B)


def moe_layer(nc, h, ident, m, combine):
    with ExitStack() as ctx:
        def sb(name, shape, dt=F32):
            return ctx.enter_context(nc.sbuf_tensor(f"moe{m.n}_{name}", shape, dt))

        wts, gslot = sb("wts", [TS, NT, m.K]), sb("gslot", [TS, NT, m.K], U32)
        te, idcols = sb("te", [1, m.M], I32), sb("idcols", [ETILE, m.M], U32)
        with nc.sbuf_tensor(f"moe{m.n}_logits", [TS, NT, m.E], F32) as lg:
            (moe0_input_phase if m.first else moe1_input_phase)(nc, h, ident, m, lg)
            routing_phase(nc, h, ident, m, lg, wts, gslot, te, idcols)
        experts_phase(nc, ident, m, te, idcols)
        combine(h, m, wts, gslot)


class Attention1:

    def __init__(self, nc, A):
        def dram(name, shape):
            return nc.dram_tensor(f"attn1_{name}", shape, F32).ap()

        self.A = {k[3:]: v for k, v in A.items() if k.startswith("a1_")}
        self.q, self.k = dram("q", (P, KC, B, SP)), dram("k", (P, KC, B, SP))
        self.v = dram("v", (TS, NT, D))
        self.pos = dram("pos", (P, 2, KC, NBK))
        self.bias = dram("bias", (B, SP, HEADS, SP))
        self.h = dram("h", (TS, NT, D))


def position_phase(nc, ident, a):
    with Phase(nc, "pos") as ph:
        sb, sem = ph.sb, ph.sem
        re, rel = sb("re", [P, D]), sb("rel", [P, D])
        gain, off = sb("gain", [P, D]), sb("off", [P, D])
        w, cols = sb("w", [P, 2, KC, D]), sb("cols", [P, 2, KC])
        st, t = sb("st", [P, 6]), sb("t", [P, 6])
        reT, pos = sb("reT", [P, KC, NBK]), sb("pos", [P, 2, KC, NBK])
        pt, pp = ph.ps("pt"), [ph.ps("pp0"), ph.ps("pp1")]
        c_in, own_v, var_ready, std_ready, re_ready, t_ps, t_ready, p_ps, pos_ready, stored = (sem(n) for n in (
            "c_in", "own_v", "var_ready", "std_ready", "re_ready", "t_ps", "t_ready", "p_ps", "pos_ready", "stored"))
        block = ph.block()

        @block.sync
        def _(sp):
            for dst, src in ((rel, a.A["rel"]), (gain, a.A["ln_g"].to_broadcast([P, D])),
                             (off, a.A["ln_b"].to_broadcast([P, D])), (w, a.A["wp"]), (cols, a.A["bp"])):
                sp.dma_start(dst[:], src).then_inc(c_in, 16)
            sp.wait_ge(pos_ready, 2)
            sp.dma_start(a.pos, pos[:]).then_inc(stored, 16)
            sp.wait_ge(stored, 16)

        @block.vector
        def _(dve):
            V = nc.vector
            own = Own(dve, own_v)
            dve.wait_ge(c_in, 16 * 5)
            own(V.bn_stats(st[:], rel[:]))
            s, d, v, qd, var, rstd = (t[:, n:n + 1] for n in range(6))
            V.tensor_tensor(s, st[:, 1:2], st[:, 4:5], ALU.add)
            V.tensor_tensor(d, st[:, 1:2], st[:, 4:5], ALU.subtract)
            own(V.tensor_tensor(v, st[:, 2:3], st[:, 5:6], ALU.add))
            V.tensor_scalar(s, s, 0.5, None, ALU.mult)
            V.tensor_scalar(v, v, 1.0 / D, EPS, ALU.mult, ALU.add)
            own(V.scalar_tensor_tensor(qd, d, 0.25, d, ALU.mult, ALU.mult))
            V.tensor_tensor(var, v, qd, ALU.add).then_inc(var_ready, 1)
            dve.wait_ge(std_ready, 1)
            own(V.reciprocal(rstd, rstd))
            own(V.tensor_scalar(re[:], rel[:], s, rstd, ALU.subtract, ALU.mult))
            own(V.tensor_tensor(re[:], re[:], gain[:], ALU.mult))
            V.tensor_tensor(re[:], re[:], off[:], ALU.add).then_inc(re_ready, 1)
            dve.wait_ge(t_ps, 1)
            V.tensor_copy(reT[:], pt[:, 0, 0:D].rearrange("p (c n) -> p c n", c=KC)).then_inc(t_ready, 1)
            for m in range(2):
                dve.wait_ge(p_ps, m + 1)
                for f in range(KC):
                    last = V.tensor_scalar(pos[:, m, f], pp[m][:, 0, f * P:(f + 1) * P], cols[:, m, f:f + 1], None, ALU.add)
                last.then_inc(pos_ready, 1)

        @block.scalar
        def _(act):
            act.wait_ge(var_ready, 1)
            nc.scalar.activation(t[:, 5:6], t[:, 4:5], ACT.Sqrt).then_inc(std_ready, 1)

        @block.tensor
        def _(pe):
            pe.wait_ge(c_in, 16 * 5)
            pe.wait_ge(re_ready, 1)
            for c in range(KC):
                last = nc.tensor.transpose(pt[:, 0, c * P:(c + 1) * P], re[:, c * P:(c + 1) * P], ident[:])
            last.then_inc(t_ps, 1)
            pe.wait_ge(t_ready, 1)
            for m in range(2):
                for f in range(KC):
                    for c in range(KC):
                        last = nc.tensor.matmul(pp[m][:, 0, f * P:(f + 1) * P], w[:, m, c, f * P:(f + 1) * P], reT[:, c],
                                                start=c == 0, stop=c == KC - 1)
                last.then_inc(p_ps, 1)


def project_phase(nc, h, ident, a, m, wts, gslot):
    with Phase(nc, "pj") as ph:
        sb, sem = ph.sb, ph.sem
        w, cols = sb("w", [P, 3, KC, D]), sb("cols", [P, 2, KC])
        vb = sb("vb", [TS, D])
        xn, xT = [sb(f"xn{q}", [TS, IT, D]) for q in range(2)], [sb(f"xT{q}", [P, KC, SP]) for q in range(2)]
        qk, v = [sb(f"qk{q}", [P, 2, KC, SP]) for q in range(2)], [sb(f"v{q}", [TS, IT, D]) for q in range(2)]
        norm, comb = ImageNorm(ph), Combine(nc, ph, m, wts, gslot)
        pt, pq, pv = ph.ps("pt", 2), ph.ps("pq", 4), ph.ps("pv", 2)
        c_in, own_v, xn_ready, xt_ps, xt_ready, q_ps, k_ps, v_ps, q_ready, k_ready, v_ready, h_out = (sem(n) for n in (
            "c_in", "own_v", "xn_ready", "xt_ps", "xt_ready", "q_ps", "k_ps", "v_ps", "q_ready", "k_ready", "v_ready", "h_out"))
        stored, added_seen = [sem(f"stored{q}") for q in range(2)], sem("added_seen")
        block = ph.block()

        @block.sync
        def _(sp):
            sp.dma_start(w[:], a.A["w"]).then_inc(c_in, 16)
            sp.dma_start(cols[:], a.A["bqk"]).then_inc(c_in, 16)
            sp.dma_start(vb[:], a.A["bv"].to_broadcast([TS, D])).then_inc(c_in, 16)
            with sp.Fori(0, B // 2) as i:
                for q in range(2):
                    b = 2 * i + q
                    sp.wait_ge(comb.added, b * IT + IT)
                    sp.dma_start(a.h[:, bass.ds(b * IT, IT)], h[:, bass.ds(b * IT, IT)]).then_inc(h_out, 16)
                    sp.wait_ge(q_ready, b + 1)
                    sp.dma_start(a.q[:, :, bass.ds(b, 1)].rearrange("p c o s -> p c (o s)"), qk[q][:, 0]).then_inc(stored[q], 16)
                    sp.wait_ge(k_ready, b + 1)
                    sp.dma_start(a.k[:, :, bass.ds(b, 1)].rearrange("p c o s -> p c (o s)"), qk[q][:, 1]).then_inc(stored[q], 16)
                    sp.wait_ge(v_ready, b + 1)
                    sp.dma_start(a.v[:, bass.ds(b * IT, IT)], v[q][:]).then_inc(stored[q], 16)
            for q in range(2):
                sp.wait_ge(stored[q], 48 * (B // 2))
            sp.wait_ge(h_out, 16 * B)

        @block.gpsimd
        def _(pool):
            comb.gathers(pool)

        @block.vector
        def _(dve):
            V = nc.vector
            own = Own(dve, own_v)

            def normalised(b, q):
                comb.add(dve, own, b, q, h)
                dve.wait_ge(comb.added, b * IT + IT)
                dve.sem_inc(added_seen, 1)
                norm.normalise(nc, dve, own, b, q, h, xn[q]).then_inc(xn_ready, 1)

            normalised(0, 0)
            dve.wait_ge(c_in, 16 * 3)

            def step(b, q, last_image):
                if not last_image:
                    free(dve, xt_ps, b)
                    normalised(b + 1, 1 - q)
                free(dve, stored[q], (b - q) * 24)
                dve.wait_ge(q_ps, b + 1)
                for f in range(KC):
                    last = V.tensor_scalar(qk[q][:, 0, f], pq[:, f, 0:SP], cols[:, 0, f:f + 1], None, ALU.add)
                last.then_inc(q_ready, 1)
                dve.wait_ge(v_ps, b + 1)
                V.tensor_tensor(v[q][:, 0:2], pv[0:TS, 0].rearrange("p (t d) -> p t d", t=2),
                                vb[:].unsqueeze(1).to_broadcast([TS, 2, D]), ALU.add)
                V.tensor_tensor(v[q][:, 2], pv[0:TS, 1, 0:D], vb[:], ALU.add).then_inc(v_ready, 1)

            pairs(own.loop(B // 2 - 2, 2 * (norm.OWN + comb.OWN * (m.K - 1)), first=1), step)

        @block.scalar
        def _(act):
            def copy_x(b, q):
                act.wait_ge(xt_ps, b + 1)
                nc.scalar.activation(xT[q][:], pt[:, :, 0:SP], ACT.Copy).then_inc(xt_ready, 1)

            def step(b, q, last_image):
                free(act, stored[q], (b - q) * 24)
                act.wait_ge(k_ps, b + 1)
                for f in range(KC):
                    last = nc.scalar.activation(qk[q][:, 1, f], pq[:, 2 + f, 0:SP], ACT.Identity, bias=cols[:, 1, f:f + 1])
                last.then_inc(k_ready, 1)
                if not last_image:
                    norm.root(nc, act, b + 1, 1 - q)
                    copy_x(b + 1, 1 - q)

            norm.root(nc, act, 0, 0)
            act.wait_ge(c_in, 16 * 3)
            copy_x(0, 0)
            pairs(act.Fori(1, B // 2 - 1), step)

        @block.tensor
        def _(pe):
            pe.wait_ge(c_in, 16 * 3)

            def transposes(b, q):
                pe.wait_ge(xn_ready, b + 1)
                transpose_image(nc, pt, xn[q], ident).then_inc(xt_ps, 1)

            def step(b, q, last_image):
                pe.wait_ge(xt_ready, b + 1)
                for n, done, out in ((0, q_ps, q_ready), (1, k_ps, k_ready)):
                    free(pe, out, b)
                    for f in range(KC):
                        for c in range(KC):
                            last = nc.tensor.matmul(pq[:, 2 * n + f, 0:SP], w[:, n, c, f * P:(f + 1) * P], xT[q][:, c, :],
                                                    start=c == 0, stop=c == KC - 1)
                    last.then_inc(done, 1)
                free(pe, v_ready, b)
                for u in range(IT):
                    for c in range(KC):
                        last = nc.tensor.matmul(pv[0:TS, u // 2, (u % 2) * D:(u % 2 + 1) * D],
                                                xT[q][:, c, u * TS:(u + 1) * TS], w[:, 2, c, :], start=c == 0, stop=c == KC - 1)
                last.then_inc(v_ps, 1)
                if not last_image:
                    transposes(b + 1, 1 - q)

            transposes(0, 0)
            pairs(pe.Fori(1, B // 2 - 1), step)


def bucket_of(dist):
    dist = np.asarray(dist)
    mid, top = SPAN // 2, 2 * SPAN
    far = np.where(np.abs(dist) < mid, mid - 1, np.abs(dist)).astype(np.float32)
    log = np.ceil(np.log(far / np.float32(mid)) / np.float32(np.log((top - 1) / mid)) * np.float32(mid - 1)) + mid
    rel = np.where(far <= mid, dist.astype(np.float32), log * np.sign(dist).astype(np.float32)).astype(np.int32)
    return np.clip(rel + SPAN, 0, NBK - 1)


def bias_phase(nc, a):
    M = B * HG
    with Phase(nc, "bi") as ph:
        sb, sem = ph.sb, ph.sem
        Dt = sb("Dt", [P, SP, NBK])
        Ct = [sb(f"Ct{q}", [P, CMAX, NBK]) for q in range(2)]
        T = [sb(f"T{q}", [P, CMAX * SP]) for q in range(2)]
        pos, hm = sb("pos", [P, 2, KC, NBK]), sb("hm", [P, HG])
        rows = [sb(f"rows{q}", [P, KC, B * CMAX]) for q in range(2)]
        spread = [sb(f"spread{q}", [P, KC, BR, M]) for q in range(2)]
        ps = [ph.ps(f"ps{n}", 2) for n in range(4)]
        c_in, spread_ready, prod_ps, out_ready, t_far, t_ready = (sem(n) for n in (
            "c_in", "spread_ready", "prod_ps", "out_ready", "t_far", "t_ready"))
        t_out = [sem(f"t_out{q}") for q in range(2)]
        rows_in = [sem(f"rows_in{q}") for q in range(2)]
        block = ph.block()
        chunks = [(k, i0, n) for k in range(2) for i0, n in CHUNKS]
        first_step = [sum(n for _, _, n in chunks[:c]) // BR for c in range(len(chunks) + 1)]

        @block.sync
        def _(sp):
            sp.dma_start(pos[:], a.pos).then_inc(c_in, 16)
            sp.dma_start(hm[:], a.A["headmask"]).then_inc(c_in, 16)

            def load(c):
                k, i0, n = chunks[c]
                if c >= 2:
                    sp.wait_ge(spread_ready, first_step[c - 1])
                for f in range(KC):
                    sp.dma_start(rows[c % 2][:, f, 0:B * n].rearrange("p (b i) -> p b i", b=B),
                                 (a.k, a.q)[k][:, f, :, i0:i0 + n]).then_inc(rows_in[c % 2], 16)

            for c in range(len(CHUNKS) + 2):
                load(c)
            for c, (i0, n) in enumerate(CHUNKS):
                if len(CHUNKS) + 2 + c < len(chunks):
                    load(len(CHUNKS) + 2 + c)
                sp.wait_ge(t_ready, c + 1)
                for f in range(KC):
                    for b in range(B):
                        p0 = f * M + b * HG
                        sp.dma_start(a.bias[b, i0:i0 + n, f * HG:(f + 1) * HG].rearrange("i h j -> h i j"),
                                     T[c % 2][p0:p0 + HG, 0:n * SP].rearrange("p (i j) -> p i j", i=n)).then_inc(t_out[c % 2], 16)
            for q in range(2):
                sp.wait_ge(t_out[q], 16 * KC * B * len(CHUNKS[q::2]))

        @block.gpsimd
        def _(pool):
            pool.wait_ge(c_in, 32)
            heads = hm[:].unsqueeze(1).unsqueeze(1).to_broadcast([P, BR, B, HG])
            for c, (k, i0, n) in enumerate(chunks):
                pool.wait_ge(rows_in[c % 2], 16 * KC * (c // 2 + 1))
                for s in range(first_step[c], first_step[c + 1]):
                    r0 = (s - first_step[c]) * BR
                    if s >= 2:
                        pool.wait_ge(prod_ps, s - 1)
                    for f in range(KC):
                        src = rows[c % 2][:, f, 0:B * n].rearrange("p (b i) -> p i b", b=B)[:, r0:r0 + BR]
                        last = nc.gpsimd.tensor_tensor(spread[s % 2][:, f].rearrange("p i (b h) -> p i b h", b=B),
                                                       src.unsqueeze(3).to_broadcast([P, BR, B, HG]), heads, ALU.mult)
                    last.then_inc(spread_ready, 1)

        @block.tensor
        def _(pe):
            pe.wait_ge(c_in, 32)
            for s in range(first_step[-1]):
                table = 0 if s >= first_step[len(CHUNKS)] else 1
                pe.wait_ge(spread_ready, s + 1)
                if s >= 4:
                    pe.wait_ge(out_ready, s - 3)
                for i in range(BR):
                    for f in range(KC):
                        last = nc.tensor.matmul(ps[s % 4][f * M:(f + 1) * M, i // 3, (i % 3) * NBK:(i % 3 + 1) * NBK],
                                                spread[s % 2][:, f, i], pos[:, table, f], start=True, stop=True)
                last.then_inc(prod_ps, 1)

        @block.scalar
        def _(act):
            for c, (k, i0, n) in enumerate(chunks):
                if k == 1:
                    free(act, t_ready, c - len(CHUNKS) - 1)
                for s in range(first_step[c], first_step[c + 1]):
                    r0 = (s - first_step[c]) * BR
                    act.wait_ge(prod_ps, s + 1)
                    dst = Ct[(c - len(CHUNKS)) % 2][:, r0:r0 + BR] if k == 1 else Dt[:, i0 + r0:i0 + r0 + BR]
                    nc.scalar.activation(dst.rearrange("p (g i) n -> p g (i n)", g=2), ps[s % 4][:, :, 0:3 * NBK],
                                         ACT.Copy).then_inc(out_ready, 1)

        @block.vector
        def _(dve):
            V = nc.vector

            def band(Tc, Cc, i0, lo, hi, d1, d2, k):
                at, m, L = (lo - i0) * SP + lo - d2, hi - lo, d2 - d1 + 1
                return V.tensor_tensor(
                    bass.AP(Tc, at, [[CMAX * SP, P], [SP + 1, m], [1, L]]),
                    Cc[:, lo - i0:hi - i0, k:k + 1].to_broadcast([P, m, L]),
                    bass.AP(Dt, (lo - d2) * NBK + k, [[SP * NBK, P], [NBK, m], [NBK, L]]), ALU.add)

            def linear(Tc, Cc, i0, n):
                d2 = SPAN // 2
                lo, hi = max(i0, d2), min(i0 + n, SP - d2)
                m, L = hi - lo, 2 * d2 + 1
                if m <= 0:
                    return None, (i0, i0)
                k = int(bucket_of(d2))
                at = (lo - i0) * SP + lo - d2
                return V.tensor_tensor(
                    bass.AP(Tc, at, [[CMAX * SP, P], [SP + 1, m], [1, L]]),
                    bass.AP(Cc, (lo - i0) * NBK + k, [[CMAX * NBK, P], [NBK, m], [-1, L]]),
                    bass.AP(Dt, (lo - d2) * NBK + k, [[SP * NBK, P], [NBK, m], [NBK - 1, L]]), ALU.add), (lo, hi)

            def diagonals(Tc, Cc, r0, n, d1, d2, i0):
                k = int(bucket_of(d1))
                lo, hi = max(r0, d2), min(r0 + n, SP + d1)
                last = band(Tc, Cc, i0, lo, hi, d1, d2, k) if lo < hi else None
                for d in range(d1, d2 + 1):
                    for a0, a1 in ((max(r0, d), min(r0 + n, lo)), (max(r0, d, hi, lo), min(r0 + n, SP + d))):
                        if a0 < a1:
                            last = band(Tc, Cc, i0, a0, a1, d, d, k)
                return last

            near = next(d for d in range(SP) if all(bucket_of(np.arange(d, SP)) == NBK - 1)
                        and all(bucket_of(-np.arange(d, SP)) == 0))
            starts = [d for d in range(-near + 1, near) if d == -near + 1 or bucket_of(d) != bucket_of(d - 1)]
            runs = list(zip(starts, [d - 1 for d in starts[1:]] + [near - 1]))
            rects = 0
            for c, (i0, n) in enumerate(CHUNKS):
                dve.wait_ge(out_ready, first_step[len(CHUNKS) + c + 1])
                free(dve, t_out[c % 2], 16 * KC * B * (c // 2))
                Tc, Cc = T[c % 2], Ct[c % 2]
                rect = Tc[:, 0:n * SP].rearrange("p (i j) -> p i j", i=n)
                for k, j0, j1 in ((NBK - 1, 0, i0 + n - near), (0, i0 + near, SP)):
                    if j1 > j0:
                        rects += 1
                        V.tensor_tensor(rect[:, :, j0:j1], Cc[:, 0:n, k:k + 1].to_broadcast([P, n, j1 - j0]),
                                        Dt[:, j0:j1, k].unsqueeze(1).to_broadcast([P, n, j1 - j0]), ALU.add).then_inc(t_far, 1)
                dve.wait_ge(t_far, rects)
                _, (lo, hi) = linear(Tc, Cc, i0, n)
                for d1, d2 in runs:
                    if abs(d1) <= SPAN // 2 and abs(d2) <= SPAN // 2:
                        for a0, a1 in ((i0, lo), (hi, i0 + n)):
                            last = (diagonals(Tc, Cc, a0, a1 - a0, d1, d2, i0) or last) if a0 < a1 else last
                    else:
                        last = diagonals(Tc, Cc, i0, n, d1, d2, i0) or last
                last.then_inc(t_ready, 1)


def attention1_phase(nc, h, ident, a):
    SCALE = 1.0 / float(np.sqrt(np.float32(3 * HD)))
    NS = IT * HEADS
    NORM, TRANS, VALUES, OUT_COPY, OUT_PROD, OUT_ADD = 2, 4, 6, 7, 8, 9
    R = 6
    with Phase(nc, "a1") as ph:
        sb, sem = ph.sb, ph.sem
        kT, v = sb("kT", [P, KC, B, SP]), sb("v", [P, IT, D + HD])
        qb = sb("qb", [P, KC, SP])
        qm = [sb(f"qm{u}", [P, HEADS, TS]) for u in range(IT)]
        bt = [sb(f"bt{u}", [TS, HEADS, SP]) for u in range(IT)]
        hm, wo = sb("hm", [P, HG]), sb("wo", [P, SLOTS, D])
        bo = sb("bo", [TS, D])
        sc, pr = [sb(f"sc{q}", [TS, S]) for q in range(R)], [sb(f"pr{q}", [TS, SP]) for q in range(R)]
        prT = [sb(f"prT{q}", [P, IT, TS]) for q in range(3)]
        nm, sm, rs = sb("nm", [TS, R]), sb("sm", [TS, R]), sb("rs", [TS, R])
        cT = sb("cT", [P, SLOTS, TS])
        pss, pst, pc = [ph.ps(f"pss{q}") for q in range(3)], [ph.ps(f"pst{q}") for q in range(2)], [ph.ps(f"pc{q}") for q in range(2)]
        po = ph.ps("po")
        c_in, q_in, qm_ready, bo_added, zeroed, o_in = (sem(n) for n in ("c_in", "q_in", "qm_ready", "bo_added", "zeroed", "o_in"))
        b_in = [sem(f"b_in{u}") for u in range(IT)]
        s_ps, s_seen, s_ready, p_ready, t_ps, t_even, t_odd, v_ps = (sem(n) for n in (
            "s_ps", "s_seen", "s_ready", "p_ready", "t_ps", "t_even", "t_odd", "v_ps"))
        n_ready, c_ready, o_ps, h_done, q_free, v_zero, v_half, r_ready = (sem(n) for n in (
            "n_ready", "c_ready", "o_ps", "h_done", "q_free", "v_zero", "v_half", "r_ready"))
        v_in = [sem(f"v_in{z}") for z in range(2)]
        block = ph.block()

        def vals(j, hd):
            return v[:, j, hd * HD:(hd + 2) * HD]

        def at(b, n, lag):
            m = n - lag
            if 0 <= m < NS:
                return b, m
            if m < 0 and not isinstance(b, int):
                return b - 1, NS + m
            return None

        def tile_end(b, n, lag):
            step = at(b, n, lag)
            return (step[0], step[1] // HEADS) if step and step[1] % HEADS == HEADS - 1 else None

        def images(eng, step):
            for n in range(NS):
                step(0, n)
            with eng.Fori(1, B) as b:
                for n in range(NS):
                    step(b, n)
            for n in range(NS, NS + OUT_ADD + 1):
                step(B - 1, n)

        @block.sync
        def _(sp):
            sp.dma_start(hm[:], a.A["headmask"]).then_inc(c_in, 16)
            sp.dma_start(kT[:], a.k).then_inc(c_in, 16)

            def load(b, u):
                sp.dma_start(bt[u][:], a.bias[bass.ds(b, 1), u * TS:(u + 1) * TS].rearrange("o i h j -> (o i) h j")).then_inc(b_in[u], 16)

            def load_q(b):
                sp.dma_start(qb[:], a.q[:, :, bass.ds(b, 1)].rearrange("p c o s -> p c (o s)")).then_inc(q_in, 16)

            def load_v(b, z):
                sp.dma_start(v[0:TS, :, z * (D // 2):(z + 1) * (D // 2)],
                             a.v[:, bass.ds(b * IT, IT), z * (D // 2):(z + 1) * (D // 2)]).then_inc(v_in[z], 16)

            load_q(0)
            load(0, 0)
            sp.wait_ge(v_zero, 1)
            for z in range(2):
                load_v(0, z)
            for dst, src in ((h, a.h), (wo, a.A["wo"]), (bo, a.A["bo"].to_broadcast([TS, D]))):
                sp.dma_start(dst[:], src).then_inc(o_in, 16)
            for u in range(1, IT):
                load(0, u)
            with sp.Fori(1, B) as b:
                sp.wait_ge(qm_ready, b * IT)
                load_q(b)
                for u in range(IT):
                    sp.wait_ge(s_ready, b * NS - NS + (u + 1) * HEADS)
                    load(b, u)
                sp.wait_ge(v_half, b)
                load_v(b, 0)
                sp.wait_ge(v_ps, b * IT)
                load_v(b, 1)

        @block.gpsimd
        def _(pool):
            for q in range(R):
                nc.gpsimd.memset(pr[q][:], 0.0).then_inc(zeroed, 1)
            for q in range(3):
                nc.gpsimd.memset(prT[q][:], 0.0).then_inc(zeroed, 1)
            nc.gpsimd.memset(v[:], 0.0).then_inc(v_zero, 1)
            pool.wait_ge(c_in, 16 * 2)

            def mask(u):
                for hd in range(HEADS):
                    last = nc.gpsimd.tensor_scalar(qm[u][:, hd], qb[:, hd // HG, u * TS:(u + 1) * TS],
                                                   hm[:, hd % HG:hd % HG + 1], 1.0, ALU.mult, ALU.mult)
                last.then_inc(qm_ready, 1)

            pool.wait_ge(q_in, 16)
            for u in range(IT):
                mask(u)
            pool.wait_ge(o_in, 16 * 3)
            nc.gpsimd.tensor_tensor(h[:], h[:], bo[:].unsqueeze(1).to_broadcast([TS, NT, D]), ALU.add).then_inc(bo_added, 1)
            with pool.Fori(1, B) as b:
                pool.wait_ge(q_in, b * 16 + 16)
                for u in range(IT):
                    pool.wait_ge(s_ps, b * NS - NS + (u + 1) * HEADS)
                    pool.sem_inc(q_free, 1)
                    mask(u)

        @block.tensor
        def _(pe):
            pe.wait_ge(c_in, 16 * 2)

            def step(b, n):
                if n < NS:
                    u, hd = n // HEADS, n % HEADS
                    if hd == 0:
                        pe.wait_ge(qm_ready, b * IT + u + 1)
                    free(pe, s_ready, b * NS + n - 2)
                    nc.tensor.matmul(pss[n % 3][0:TS, 0, 0:S], qm[u][:, hd],
                                     kT[:, hd // HG, bass.ds(b, 1), 0:S].rearrange("p o s -> p (o s)"),
                                     start=True, stop=True).then_inc(s_ps, 1)
                if at(b, n, TRANS):
                    e, m = at(b, n, TRANS)
                    pe.wait_ge(n_ready, e * NS + m + 1)
                    free(pe, (t_even, t_odd)[m % 2], e * (NS // 2) + m // 2)
                    for j in range(IT):
                        last = nc.tensor.transpose(pst[m % 2][0:TS, 0, j * TS:(j + 1) * TS],
                                                   pr[m % R][:, j * TS:(j + 1) * TS], ident[0:TS, 0:TS])
                    last.then_inc(t_ps, 1)
                if at(b, n, VALUES):
                    e, m = at(b, n, VALUES)
                    u, hd = m // HEADS, m % HEADS
                    slot, g = hd % SLOTS, hd // SLOTS
                    pe.wait_ge((t_even, t_odd)[m % 2], e * (NS // 2) + m // 2 + 1)
                    if hd == 0:
                        free(pe, c_ready, e * IT + u - (0, 2, 1)[u])
                    if u == 0 and hd in (0, HEADS // 2 - 1):
                        pe.wait_ge(v_in[hd > 0], e * 16 + 16)
                    for j in range(IT):
                        last = nc.tensor.matmul(pc[u % 2][slot * 2 * HD:(slot + 1) * 2 * HD, 0, g * TS:(g + 1) * TS],
                                                vals(j, hd), prT[m % 3][:, j], start=j == 0, stop=j == IT - 1)
                    if hd == HEADS - 1:
                        last.then_inc(v_ps, 1)
                    if u == IT - 1 and hd == HEADS // 2 - 1:
                        last.then_inc(v_half, 1)
                if tile_end(b, n, OUT_PROD):
                    e, u = tile_end(b, n, OUT_PROD)
                    pe.wait_ge(c_ready, e * IT + u + 1)
                    free(pe, h_done, e * IT + u)
                    if isinstance(b, int):
                        pe.wait_ge(o_in, 16 * 3)
                    for g in range(SLOTS):
                        last = nc.tensor.matmul(po[0:TS, 0, 0:D], cT[:, g], wo[:, g], start=g == 0, stop=g == SLOTS - 1)
                    last.then_inc(o_ps, 1)

            images(pe, step)

        @block.vector
        def _(dve):
            V = nc.vector
            dve.wait_ge(c_in, 16 * 2)
            dve.wait_ge(zeroed, R + 3)

            def step(b, n):
                if at(b, n, NORM):
                    e, m = at(b, n, NORM)
                    dve.wait_ge(p_ready, e * NS + m + 1)
                    V.reciprocal(rs[:, m % R:m % R + 1], sm[:, m % R:m % R + 1]).then_inc(r_ready, 1)
                if n < NS:
                    u, hd, q = n // HEADS, n % HEADS, n % R
                    if hd == 0:
                        dve.wait_ge(b_in[u], b * 16 + 16)
                    dve.wait_ge(s_ps, b * NS + n + 1)
                    dve.sem_inc(s_seen, 1)
                    V.tensor_tensor_reduce(out=sc[q][:], in0=pss[n % 3][0:TS, 0, 0:S], in1=bt[u][:, hd, 0:S], scale=-SCALE,
                                           scalar=3e38, op0=ALU.add, op1=ALU.min, accum_out=nm[:, q:q + 1]).then_inc(s_ready, 1)
                if at(b, n, TRANS) and at(b, n, TRANS)[1] % 2:
                    e, m = at(b, n, TRANS)
                    dve.wait_ge(t_ps, e * NS + m + 1)
                    V.tensor_copy(prT[m % 3][0:TS].rearrange("p j i -> p (j i)"), pst[1][0:TS, 0, 0:SP]).then_inc(t_odd, 1)
                if at(b, n, NORM):
                    e, m = at(b, n, NORM)
                    q = m % R
                    dve.wait_ge(r_ready, e * NS + m + 1)
                    V.tensor_scalar(pr[q][:, 0:S], pr[q][:, 0:S], rs[:, q:q + 1], None, ALU.mult).then_inc(n_ready, 1)
                if tile_end(b, n, OUT_COPY):
                    e, u = tile_end(b, n, OUT_COPY)
                    dve.wait_ge(v_ps, e * IT + u + 1)
                    V.tensor_copy(cT[:].rearrange("p g s -> p (g s)"), pc[u % 2][:, 0, 0:SLOTS * TS]).then_inc(c_ready, 1)
                if tile_end(b, n, OUT_ADD):
                    e, u = tile_end(b, n, OUT_ADD)
                    t = e * IT + u
                    if isinstance(b, int):
                        dve.wait_ge(bo_added, 1)
                    dve.wait_ge(o_ps, t + 1)
                    V.tensor_tensor(h[:, t, :], po[0:TS, 0, 0:D], h[:, t, :], ALU.add).then_inc(h_done, 1)

            images(dve, step)
            dve.wait_ge(h_done, B * IT)

        @block.scalar
        def _(act):
            act.wait_ge(zeroed, R + 3)

            def step(b, n):
                if at(b, n, TRANS) and at(b, n, TRANS)[1] % 2 == 0:
                    e, m = at(b, n, TRANS)
                    act.wait_ge(t_ps, e * NS + m + 1)
                    nc.scalar.activation(prT[m % 3][0:TS].rearrange("p j i -> p (j i)"), pst[0][0:TS, 0, 0:SP], ACT.Copy).then_inc(t_even, 1)
                if n < NS:
                    q = n % R
                    act.wait_ge(s_ready, b * NS + n + 1)
                    nc.scalar.activation(pr[q][:, 0:S], sc[q][:], ACT.Exp, bias=nm[:, q:q + 1], scale=-1.0,
                                         accum_out=sm[:, q:q + 1]).then_inc(p_ready, 1)

            images(act, step)


def build(nc, A, out):
    with nc.sbuf_tensor("ident", [P, P], F32) as ident:
        constants_phase(nc, ident)
        a = Attention1(nc, A)
        with nc.sbuf_tensor("h", [TS, NT, D], F32) as h:
            s4_phase(nc, h, ident, A)
            attention0_phase(nc, h, ident, A)
            moe_layer(nc, h, ident, Moe(nc, A, 0, E0, K0),
                      lambda h, m, wts, gslot: project_phase(nc, h, ident, a, m, wts, gslot))
            position_phase(nc, ident, a)
        bias_phase(nc, a)
        with nc.sbuf_tensor("h_again", [TS, NT, D], F32) as h:
            attention1_phase(nc, h, ident, a)
            moe_layer(nc, h, ident, Moe(nc, A, 1, E1, K1),
                      lambda h, m, wts, gslot: output_phase(nc, h, m, wts, gslot, out))


def layout(i):
    a = {}

    def states(v):
        return v.reshape(2, 128, STATES).transpose(0, 2, 1).reshape(P, 128)

    ldt = np.broadcast_to(i["L0_tok_log_dt"].reshape(2, 1, 128), (2, STATES, 128)).reshape(P, 128)
    Bri = i["L0_tok_B_ri"]
    a["s4_params"] = np.stack([ldt, states(i["L0_tok_inv_A_real"]), states(i["L0_tok_A_imag"]),
                               states(Bri[..., 0]), states(Bri[..., 1])], axis=1)
    a["s4_c"] = i["x"].reshape(B, 2, 128, STATES, 2).transpose(1, 3, 4, 0, 2).reshape(P, 2, B, 128)
    a["cls"] = i["cls_tok"].reshape(D // STATES, STATES).T

    def rows(w):
        return w.reshape(KC, P, -1).transpose(1, 0, 2)

    a["a0_w"] = np.stack([rows(i["L0_attn_w_q"]), rows(i["L0_attn_w_k"]), rows(i["L0_attn_w_v"])], axis=1)

    pre = "L1_attn_"
    a["a1_w"] = np.stack([rows(i[pre + n]) for n in ("Wq", "Wk", "Wv")], axis=1)
    a["a1_bqk"] = np.stack([i[pre + n].reshape(KC, P).T for n in ("bq", "bk")], axis=1)
    a["a1_bv"], a["a1_bo"] = i[pre + "bv"][None], i[pre + "bo"][None]
    wo = i[pre + "Wo"].reshape(HEADS // SLOTS, SLOTS, HD, D).transpose(1, 2, 0, 3)
    a["a1_wo"] = np.concatenate([wo, np.zeros_like(wo)], axis=1).reshape(P, HEADS // SLOTS, D)
    a["a1_wp"] = np.stack([rows(i[pre + n]) for n in ("Wpk", "Wpq")], axis=1)
    a["a1_bp"] = np.stack([i[pre + n].reshape(KC, P).T for n in ("bpk", "bpq")], axis=1)
    a["a1_ln_g"], a["a1_ln_b"] = i[pre + "ln_g"][None], i[pre + "ln_b"][None]
    a["a1_rel"] = i[pre + "rel_emb"]
    a["a1_headmask"] = (np.arange(P)[:, None] // HD == np.arange(HG)[None]).astype(np.float32)

    for n, E, K, pre in ((0, E0, K0, "L0_ffn_"), (1, E1, K1, "L1_ffn_")):
        M = expert_tiles(E, K)
        a[f"m{n}_gate"] = rows(i[pre + "gate_w"].T)
        desc = np.float32(E) - np.arange(E, dtype=np.float32)
        a[f"m{n}_desc"] = np.tile(desc, (TS, 1))
        real = np.ones((TS, NT), np.float32)
        real[TS - 1, IT - 1::IT] = 0.0
        a[f"m{n}_real"] = real
        pad = np.zeros((TS, NT, K), np.float32)
        pad[TS - 1, IT - 1::IT, :] = M * ETILE + np.arange(B * K, dtype=np.float32).reshape(B, K)
        a[f"m{n}_padslot"] = pad
        a[f"m{n}_tile_no"] = np.arange(M, dtype=np.float32)[None]
        a[f"m{n}_tri"] = np.triu(np.ones((TS, TS), np.float32), 1)
        rounds = -(-NT * TS * K // P)
        tok = np.arange(NT)[None, :, None] * TS + np.arange(TS)[:, None, None] + np.zeros((1, 1, K), int)
        tail = rounds * P - tok.size
        a[f"m{n}_tok"] = np.concatenate([tok.ravel(), np.zeros(tail, int)]).reshape(P, rounds).astype(np.uint32)
        a[f"m{n}_tail"] = (M * ETILE + B * K + np.arange(tail, dtype=np.uint32))[None].astype(np.uint32)
        if n == 0:
            W1, W2 = i[pre + "fc1_w"], i[pre + "fc2_w"]
            b1 = i[pre + "fc1_b"].reshape(E, 2, KC, P)
            mult = i[pre + "geglu_mult"].reshape(E, 1, KC, P)
            a["m0_b2"] = np.concatenate([i[pre + "fc2_b"], i[pre + "s_fc2_b"][None]], axis=0)
            a["m0_s_w1"] = rows(i[pre + "s_fc1_w"].T)
            a["m0_s_w2"] = i[pre + "s_fc2_w"].T.reshape(FS // P, P, D).transpose(1, 0, 2)
            a["m0_s_cols"] = np.concatenate([i[pre + "s_fc1_b"].reshape(2, FS // P, P),
                                             i[pre + "s_geglu_mult"].reshape(1, FS // P, P)]).transpose(2, 0, 1)
        else:
            W1 = np.concatenate([i[pre + "w1"][:, 1::2], i[pre + "w1"][:, 0::2]], axis=1)
            W2 = i[pre + "w2"]
            b1 = np.stack([i[pre + "b1"][:, 1::2], i[pre + "b1"][:, 0::2]], axis=1).reshape(E, 2, KC, P)
            mult = np.zeros((E, 1, KC, P), np.float32)
            a["m1_b2"] = i[pre + "b2"]
            a["m1_scale"] = i[pre + "norm_scale"][None]
            a["m1_gate_b"] = i[pre + "gate_b"][None]
        up = W1.transpose(0, 2, 1).reshape(E, KC, P, 2 * F).transpose(0, 2, 1, 3).reshape(E, P, KC * 2 * F)
        down = W2.transpose(0, 2, 1).reshape(E, KC, P, D).transpose(0, 2, 1, 3).reshape(E, P, KC * D)
        cols = np.concatenate([b1, mult], axis=1).reshape(E, 3 * KC, P).transpose(0, 2, 1)
        a[f"m{n}_w"] = np.concatenate([up, down, cols], axis=2)
    return {k: np.ascontiguousarray(v) for k, v in a.items()}


def kernel(**inputs):
    import concourse.bacc as bacc
    from concourse.bass_utils import run_bass_kernel_spmd

    arrays = layout({k: np.asarray(v) for k, v in inputs.items()})
    nc = bacc.Bacc("TRN2", target_bir_lowering=False, num_devices=1)
    A = {k: nc.dram_tensor(f"in_{k}", v.shape, mybir.dt.from_np(v.dtype), kind="ExternalInput").ap()
         for k, v in arrays.items()}
    out = nc.dram_tensor("out", (B, S, D), F32, kind="ExternalOutput").ap()
    build(nc, A, out)
    r = run_bass_kernel_spmd(nc, [{f"in_{k}": v for k, v in arrays.items()}], core_ids=[0])
    return r.results[0]["out"]
```
